# Optimizing a Trainium2 kernel written in Bass

```python
import numpy as np
import jax
import jax.numpy as jnp

def _softmax(x, axis=-1):
    return jax.nn.softmax(x, axis=axis)

def _gelu(x):
    return jax.nn.gelu(x, approximate=True)

def _silu(x):
    return jax.nn.silu(x)

def _sigmoid(x):
    return jax.nn.sigmoid(x)

def _layernorm(x, axis=-1, eps=1e-05):
    m = jnp.mean(x, axis=axis, keepdims=True)
    v = jnp.var(x, axis=axis, keepdims=True)
    return (x - m) / jnp.sqrt(v + eps)

def _scatter_add(tgt, idx, src, axis=0):
    return tgt.at[idx].add(src)

def _segment_sum(src, seg, n):
    return jax.ops.segment_sum(src, seg, n)
kernel_name = 'mk_xattn_seq_d2_seqx_r8_b2945f'

def setup_inputs(seed: int=0):
    np.random.seed(seed)
    _w = jnp.asarray

    def _rec_inputs():
        import jax
        import jax.numpy as jnp
        _rk = jax.random.key(seed)
        x = -0.0002928 + 1 * jax.random.normal(jax.random.fold_in(_rk, 1), (16, 128, 128), jnp.float32)
        _lenS = 128 - jax.random.randint(jax.random.fold_in(_rk, 7), (16,), 0, max(1, 128 // 4) + 1, jnp.int32)
        _lenS2 = 77 - jax.random.randint(jax.random.fold_in(_rk, 8), (16,), 0, max(1, 77 // 4) + 1, jnp.int32)
        _ctx_1024P = jax.random.normal(jax.random.fold_in(_rk, 11), (16, 16, 128), jnp.float32)
        _ctx_1024c = jax.random.dirichlet(jax.random.fold_in(_rk, 511), 0.3 * jnp.ones((16,), jnp.float32), (16, 77))
        _ctx_1024t = jnp.einsum('bsk,bkd->bsd', _ctx_1024c, _ctx_1024P)
        _ctx_1024t = _ctx_1024t * jax.lax.rsqrt(jnp.mean(jnp.square(_ctx_1024t)) + 1e-12) * 0.953939
        ctx_1024 = -1.39393e-06 + 0.999914 * (_ctx_1024t + 0.3 * jax.random.normal(jax.random.fold_in(_rk, 611), (16, 77, 128), jnp.float32))
        _validS = jnp.arange(128)[None, :] < _lenS[:, None]
        _validS2 = jnp.arange(77)[None, :] < _lenS2[:, None]
        _causal = jnp.tril(jnp.ones((128, 128), dtype=bool))
        mask_1x1xSxS_ik0 = jnp.where(jnp.broadcast_to(_validS[0:1, None, None, :], (1, 1, 128, 128)), 0, 1).astype(jnp.int32)
        return (x, ctx_1024, mask_1x1xSxS_ik0)
    x, ctx_1024, mask_1x1xSxS_ik0 = _rec_inputs()

    def _L0_xattn_setup():
        import jax, jax.numpy as jnp
        import numpy as np
        D_MODEL = 128
        NHEAD = 16
        D_FF = 512
        B = 2
        S = 256
        EPS = 1e-05

        def _mha(q_in, k_in, v_in, qw, qb, kw, kb, vw, vb, ow, ob, mask):
            b, sq, d = q_in.shape
            sk = k_in.shape[1]
            hd = d // NHEAD
            q = (q_in @ qw + qb).reshape(b, sq, NHEAD, hd).transpose(0, 2, 1, 3)
            k = (k_in @ kw + kb).reshape(b, sk, NHEAD, hd).transpose(0, 2, 1, 3)
            v = (v_in @ vw + vb).reshape(b, sk, NHEAD, hd).transpose(0, 2, 1, 3)
            scores = jnp.einsum('bhqd,bhkd->bhqk', q, k) / jnp.sqrt(jnp.float32(hd))
            if mask is not None:
                scores = jnp.where(mask == 0, jnp.float32(-1000000000.0), scores)
            attn = jax.nn.softmax(scores, axis=-1)
            out = jnp.einsum('bhqk,bhkd->bhqd', attn, v)
            out = out.transpose(0, 2, 1, 3).reshape(b, sq, d)
            return out @ ow + ob

        def _layernorm(x, g, b):
            mu = jnp.mean(x, axis=-1, keepdims=True)
            var = jnp.var(x, axis=-1, keepdims=True)
            return (x - mu) * jax.lax.rsqrt(var + EPS) * g + b
        key = jax.random.key(seed)
        ks = jax.random.split(key, 16)
        sc = 0.02
        inp = {'tgt': jax.random.normal(ks[0], (B, S, D_MODEL), jnp.float32), 'memory': jax.random.normal(ks[1], (B, S, D_MODEL), jnp.float32), 'tgt_mask': jnp.tril(jnp.ones((S, S), jnp.int32))[None, None, :, :], 'sa_qw': jax.random.normal(ks[2], (D_MODEL, D_MODEL), jnp.float32) * sc, 'sa_qb': jnp.zeros((D_MODEL,), jnp.float32), 'sa_kw': jax.random.normal(ks[3], (D_MODEL, D_MODEL), jnp.float32) * sc, 'sa_kb': jnp.zeros((D_MODEL,), jnp.float32), 'sa_vw': jax.random.normal(ks[4], (D_MODEL, D_MODEL), jnp.float32) * sc, 'sa_vb': jnp.zeros((D_MODEL,), jnp.float32), 'sa_ow': jax.random.normal(ks[5], (D_MODEL, D_MODEL), jnp.float32) * sc, 'sa_ob': jnp.zeros((D_MODEL,), jnp.float32), 'ca_qw': jax.random.normal(ks[6], (D_MODEL, D_MODEL), jnp.float32) * sc, 'ca_qb': jnp.zeros((D_MODEL,), jnp.float32), 'ca_kw': jax.random.normal(ks[7], (D_MODEL, D_MODEL), jnp.float32) * sc, 'ca_kb': jnp.zeros((D_MODEL,), jnp.float32), 'ca_vw': jax.random.normal(ks[8], (D_MODEL, D_MODEL), jnp.float32) * sc, 'ca_vb': jnp.zeros((D_MODEL,), jnp.float32), 'ca_ow': jax.random.normal(ks[9], (D_MODEL, D_MODEL), jnp.float32) * sc, 'ca_ob': jnp.zeros((D_MODEL,), jnp.float32), 'w1': jax.random.normal(ks[10], (D_MODEL, D_FF), jnp.float32) * sc, 'b1': jnp.zeros((D_FF,), jnp.float32), 'w2': jax.random.normal(ks[11], (D_FF, D_MODEL), jnp.float32) * sc, 'b2': jnp.zeros((D_MODEL,), jnp.float32), 'g1': jnp.ones((D_MODEL,), jnp.float32), 'be1': jnp.zeros((D_MODEL,), jnp.float32), 'g2': jnp.ones((D_MODEL,), jnp.float32), 'be2': jnp.zeros((D_MODEL,), jnp.float32), 'g3': jnp.ones((D_MODEL,), jnp.float32), 'be3': jnp.zeros((D_MODEL,), jnp.float32)}
        return inp
    _L0_xattn_all = _L0_xattn_setup()
    _L0_xattn_in = {k: v for k, v in _L0_xattn_all.items() if k in ('sa_qw', 'sa_qb', 'sa_kw', 'sa_kb', 'sa_vw', 'sa_vb', 'sa_ow', 'sa_ob', 'ca_qw', 'ca_qb', 'ca_kw', 'ca_kb', 'ca_vw', 'ca_vb', 'ca_ow', 'ca_ob', 'w1', 'b1', 'w2', 'b2', 'g1', 'be1', 'g2', 'be2', 'g3', 'be3')}
    del _L0_xattn_all

    def _L1_xattn_setup():
        import jax, jax.numpy as jnp
        import numpy as np
        LN_EPS = 1e-05
        ATTN_EPS = 1e-06
        key = jax.random.key(seed)
        k1, k2, k3 = jax.random.split(key, 3)
        B, Nq, Nk, D = (8, 256, 256, 128)
        return {'query': jax.random.normal(k1, (B, Nq, D), dtype=jnp.float32), 'key': jax.random.normal(k2, (B, Nk, D), dtype=jnp.float32), 'value': jax.random.normal(k3, (B, Nk, D), dtype=jnp.float32), 'gamma': jnp.ones((D,), dtype=jnp.float32), 'beta': jnp.zeros((D,), dtype=jnp.float32)}
    _L1_xattn_all = _L1_xattn_setup()
    _L1_xattn_in = {k: v for k, v in _L1_xattn_all.items() if k in ('gamma', 'beta')}
    del _L1_xattn_all
    return {'x': x, 'ctx_1024': ctx_1024, 'mask_1x1xSxS_ik0': mask_1x1xSxS_ik0, 'L0_xattn_sa_qw': _L0_xattn_in['sa_qw'], 'L0_xattn_sa_qb': _L0_xattn_in['sa_qb'], 'L0_xattn_sa_kw': _L0_xattn_in['sa_kw'], 'L0_xattn_sa_kb': _L0_xattn_in['sa_kb'], 'L0_xattn_sa_vw': _L0_xattn_in['sa_vw'], 'L0_xattn_sa_vb': _L0_xattn_in['sa_vb'], 'L0_xattn_sa_ow': _L0_xattn_in['sa_ow'], 'L0_xattn_sa_ob': _L0_xattn_in['sa_ob'], 'L0_xattn_ca_qw': _L0_xattn_in['ca_qw'], 'L0_xattn_ca_qb': _L0_xattn_in['ca_qb'], 'L0_xattn_ca_kw': _L0_xattn_in['ca_kw'], 'L0_xattn_ca_kb': _L0_xattn_in['ca_kb'], 'L0_xattn_ca_vw': _L0_xattn_in['ca_vw'], 'L0_xattn_ca_vb': _L0_xattn_in['ca_vb'], 'L0_xattn_ca_ow': _L0_xattn_in['ca_ow'], 'L0_xattn_ca_ob': _L0_xattn_in['ca_ob'], 'L0_xattn_w1': _L0_xattn_in['w1'], 'L0_xattn_b1': _L0_xattn_in['b1'], 'L0_xattn_w2': _L0_xattn_in['w2'], 'L0_xattn_b2': _L0_xattn_in['b2'], 'L0_xattn_g1': _L0_xattn_in['g1'], 'L0_xattn_be1': _L0_xattn_in['be1'], 'L0_xattn_g2': _L0_xattn_in['g2'], 'L0_xattn_be2': _L0_xattn_in['be2'], 'L0_xattn_g3': _L0_xattn_in['g3'], 'L0_xattn_be3': _L0_xattn_in['be3'], 'L1_xattn_gamma': _L1_xattn_in['gamma'], 'L1_xattn_beta': _L1_xattn_in['beta']}

def reference(x, ctx_1024, mask_1x1xSxS_ik0, L0_xattn_sa_qw, L0_xattn_sa_qb, L0_xattn_sa_kw, L0_xattn_sa_kb, L0_xattn_sa_vw, L0_xattn_sa_vb, L0_xattn_sa_ow, L0_xattn_sa_ob, L0_xattn_ca_qw, L0_xattn_ca_qb, L0_xattn_ca_kw, L0_xattn_ca_kb, L0_xattn_ca_vw, L0_xattn_ca_vb, L0_xattn_ca_ow, L0_xattn_ca_ob, L0_xattn_w1, L0_xattn_b1, L0_xattn_w2, L0_xattn_b2, L0_xattn_g1, L0_xattn_be1, L0_xattn_g2, L0_xattn_be2, L0_xattn_g3, L0_xattn_be3, L1_xattn_gamma, L1_xattn_beta):
    import jax
    import jax.numpy as jnp

    def _L0_xattn_ref(tgt, memory, tgt_mask, sa_qw, sa_qb, sa_kw, sa_kb, sa_vw, sa_vb, sa_ow, sa_ob, ca_qw, ca_qb, ca_kw, ca_kb, ca_vw, ca_vb, ca_ow, ca_ob, w1, b1, w2, b2, g1, be1, g2, be2, g3, be3):
        import jax, jax.numpy as jnp
        import numpy as np
        D_MODEL = 128
        NHEAD = 16
        D_FF = 512
        B = 2
        S = 256
        EPS = 1e-05

        def _mha(q_in, k_in, v_in, qw, qb, kw, kb, vw, vb, ow, ob, mask):
            b, sq, d = q_in.shape
            sk = k_in.shape[1]
            hd = d // NHEAD
            q = (q_in @ qw + qb).reshape(b, sq, NHEAD, hd).transpose(0, 2, 1, 3)
            k = (k_in @ kw + kb).reshape(b, sk, NHEAD, hd).transpose(0, 2, 1, 3)
            v = (v_in @ vw + vb).reshape(b, sk, NHEAD, hd).transpose(0, 2, 1, 3)
            scores = jnp.einsum('bhqd,bhkd->bhqk', q, k) / jnp.sqrt(jnp.float32(hd))
            if mask is not None:
                scores = jnp.where(mask == 0, jnp.float32(-1000000000.0), scores)
            attn = jax.nn.softmax(scores, axis=-1)
            out = jnp.einsum('bhqk,bhkd->bhqd', attn, v)
            out = out.transpose(0, 2, 1, 3).reshape(b, sq, d)
            return out @ ow + ob

        def _layernorm(x, g, b):
            mu = jnp.mean(x, axis=-1, keepdims=True)
            var = jnp.var(x, axis=-1, keepdims=True)
            return (x - mu) * jax.lax.rsqrt(var + EPS) * g + b
        x = tgt + _mha(tgt, tgt, tgt, sa_qw, sa_qb, sa_kw, sa_kb, sa_vw, sa_vb, sa_ow, sa_ob, tgt_mask)
        x = _layernorm(x, g1, be1)
        x = x + _mha(x, memory, memory, ca_qw, ca_qb, ca_kw, ca_kb, ca_vw, ca_vb, ca_ow, ca_ob, None)
        x = _layernorm(x, g2, be2)
        x = x + (jax.nn.relu(x @ w1 + b1) @ w2 + b2)
        x = _layernorm(x, g3, be3)
        return x

    def _L1_xattn_ref(query, key, value, gamma, beta):
        import jax, jax.numpy as jnp
        import numpy as np
        LN_EPS = 1e-05
        ATTN_EPS = 1e-06
        Q_phi = jax.nn.elu(query)
        K_phi = jax.nn.elu(key)
        KV = jnp.einsum('bnd,bne->bde', K_phi, value)
        Z = 1.0 / (jnp.einsum('bnd,bd->bn', Q_phi, K_phi.sum(axis=1)) + ATTN_EPS)
        attn = jnp.einsum('bnd,bde->bne', Q_phi, KV) * Z[..., None]
        x = query + attn
        mean = jnp.mean(x, axis=-1, keepdims=True)
        var = jnp.mean(jnp.square(x - mean), axis=-1, keepdims=True)
        return (x - mean) * jax.lax.rsqrt(var + LN_EPS) * gamma + beta
    x = _L0_xattn_ref(x, ctx_1024, mask_1x1xSxS_ik0, L0_xattn_sa_qw, L0_xattn_sa_qb, L0_xattn_sa_kw, L0_xattn_sa_kb, L0_xattn_sa_vw, L0_xattn_sa_vb, L0_xattn_sa_ow, L0_xattn_sa_ob, L0_xattn_ca_qw, L0_xattn_ca_qb, L0_xattn_ca_kw, L0_xattn_ca_kb, L0_xattn_ca_vw, L0_xattn_ca_vb, L0_xattn_ca_ow, L0_xattn_ca_ob, L0_xattn_w1, L0_xattn_b1, L0_xattn_w2, L0_xattn_b2, L0_xattn_g1, L0_xattn_be1, L0_xattn_g2, L0_xattn_be2, L0_xattn_g3, L0_xattn_be3)
    x = _L1_xattn_ref(x, ctx_1024, ctx_1024, L1_xattn_gamma, L1_xattn_beta)
    return x

_drawn_inputs = setup_inputs


def setup_inputs(seed=0):
    import zlib

    import numpy as np

    out = dict(_drawn_inputs(seed))
    spreads = {'L0_xattn_sa_qb': (0.0, 0.8),
     'L0_xattn_sa_kb': (0.0, 0.8),
     'L0_xattn_sa_vb': (0.0, 0.1),
     'L0_xattn_sa_ob': (0.0, 0.1),
     'L0_xattn_ca_qb': (0.0, 0.8),
     'L0_xattn_ca_kb': (0.0, 0.8),
     'L0_xattn_ca_vb': (0.0, 0.1),
     'L0_xattn_ca_ob': (0.0, 0.1),
     'L0_xattn_b1': (0.0, 0.1),
     'L0_xattn_b2': (0.0, 0.1),
     'L0_xattn_g1': (1.0, 0.2),
     'L0_xattn_be1': (0.0, 0.1),
     'L0_xattn_g2': (1.0, 0.2),
     'L0_xattn_be2': (0.0, 0.1),
     'L0_xattn_g3': (1.0, 0.2),
     'L0_xattn_be3': (0.0, 0.1),
     'L1_xattn_gamma': (1.0, 0.2),
     'L1_xattn_beta': (0.0, 0.1)}
    factors = {'L0_xattn_sa_qw': 8.0, 'L0_xattn_sa_kw': 8.0, 'L0_xattn_ca_qw': 8.0, 'L0_xattn_ca_kw': 8.0}
    for name, (base, spread) in spreads.items():
        noise = np.random.default_rng([zlib.crc32(name.encode()), seed]).standard_normal(out[name].shape)
        drawn = base * np.exp(spread * noise) if base else spread * noise
        out[name] = jnp.asarray(drawn.astype(out[name].dtype))
    for name, factor in factors.items():
        out[name] = (out[name] * factor).astype(out[name].dtype)
    return out
```

```python
from contextlib import ExitStack

import concourse.bass as bass
from concourse import mybir

F32 = mybir.dt.float32
BF16 = mybir.dt.bfloat16
I32 = mybir.dt.int32
ALU = mybir.AluOpType
ACT = mybir.ActivationFunctionType
AX_X = mybir.AxisListType.X

P = 128
NH = 16
HD = 8
UNITS = 4
RH = 4
G = 2
MASKED = -float(2 ** 32)
SLOT_DMAS = 2 * 4 * RH
LN_EPS = 1e-5
DEN_EPS = 1e-6
VW = 32

C_SQB, C_SKB, C_CQB, C_CKB, C_B1, C_G1, C_E1, C_G2, C_E2, C_G3, C_E3 = 0, 1, 2, 3, 4, 8, 9, 10, 11, 12, 13
N_COLS = 14
R_SVB, R_SOB, R_CVB, R_COB, R_B2, R_G1, R_E1, R_G2, R_E2, R_G3, R_E3, R_GAM, R_BET = range(13)
N_ROWS = 13
W_SQ, W_SK, W_SV, W_SO, W_CQ, W_CK, W_CV, W_CO, W_1, W_2 = 0, 1, 2, 3, 4, 5, 6, 7, 8, 12
N_W = 16


def decoder_layer_kernel(nc, x, x_t, ctx_n, ctx_t, mask_q, mask_k, weights, cols, rows, ident, out):
    B, S, D = x.shape
    SK = ctx_n.shape[1]
    NG = B // G
    NF = 4
    SCALE = 1.0 / float(HD) ** 0.5
    KLEN = {"s": S, "c": SK}

    NEXT, SELF, CROSS, TAIL = -1, 0, 1, 2

    def static(i):
        return isinstance(i, int)

    def on(i, first):
        return 0 <= i - first < NG if static(i) else True

    def begun(i, first):
        return min(max(i - first, 0), NG) if static(i) else i - first

    def count(i, firsts, at):
        if static(i):
            return sum(begun(i, f) for f in firsts) + sum(int(on(i, f)) for f in firsts[:at])
        return i * len(firsts) + (at - sum(firsts))

    JOB_STAGES = [SELF, SELF, CROSS, CROSS]

    def job_index(i, k):
        return count(i, JOB_STAGES, k)

    def schedule(i, k):
        def job(at, back=0):
            if at >= 4:
                return job(at - 4, back - 1)
            if at < 0:
                return job(at + 4, back + 1)
            first = JOB_STAGES[at]
            if not on(i - back, first):
                return None
            return ("s" if first == SELF else "c", at % 2, i - back - first, job_index(i - back, at))
        return job(k), job(k + 1), job(k - 1), job(k - 2)

    PROJ_USES = [("cv", CROSS), ("h01", TAIL), ("h23", TAIL), ("ff", TAIL), ("sqk", NEXT), ("sv", NEXT), ("kv", TAIL),
                 ("yt", TAIL), ("cqk", SELF), ("la", TAIL)]

    def use_index(i, name):
        return count(i, [f for _, f in PROJ_USES], [n for n, _ in PROJ_USES].index(name))

    def wait_reuse(eng, sem, value):
        if not static(value) or value > 0:
            eng.wait_ge(sem, value)

    def run_iterations(eng, iteration):
        for i in range(NEXT, TAIL):
            iteration(i)
        with eng.Fori(TAIL, NG - 1) as i:
            iteration(i)
        for i in range(NG - 1, NG + TAIL):
            iteration(i)

    with ExitStack() as ctx:
        def sb(name, shape, dt=F32):
            return ctx.enter_context(nc.sbuf_tensor(name, shape, dt))

        def psum(name, shape, dt=F32):
            return ctx.enter_context(nc.psum_tensor(name, shape, dt))

        def sem(name):
            return ctx.enter_context(nc.semaphore(name))

        w_sb = sb("w_sb", [P, N_W, P])
        col_sb = sb("col_sb", [P, N_COLS])
        row_sb = sb("row_sb", [P, N_ROWS, P])
        id_f = sb("id_f", [P, P])
        id_b = sb("id_b", [P, P], BF16)
        head_sel = sb("head_sel", [P, NH, P], BF16)
        ones_b = sb("ones_b", [P, P], BF16)
        mask_q_i = sb("mask_q_i", [P, S], I32)
        mask_k_i = sb("mask_k_i", [P, S], I32)
        bias_q = sb("bias_q", [P, S], BF16)
        bias_k = sb("bias_k", [P, S], BF16)
        keep_k = sb("keep_k", [P, S], BF16)
        any_key = sb("any_key", [P, S])
        neg_half = sb("neg_half", [P, G])
        res_bias = sb("res_bias", [P, 2, P])
        x_all = sb("x_all", [P, B, D])
        r0 = sb("r0", [P, B, D])
        r1 = sb("r1", [P, B, D])
        r2 = sb("r2", [P, B, D])
        r3 = sb("r3", [P, B, D])
        o_all = sb("o_all", [P, B, D])
        xt_in = sb("xt_in", [P, G, S])
        ct_in = sb("ct_in", [P, G, SK])
        cn_in = sb("cn_in", [SK, G, D + 1])
        split = {}
        for kind in "sc":
            for side in "qk":
                n = KLEN[kind] if side == "k" else S
                split[kind, side] = (sb(f"{kind}{side}_f", [P, G, n]), sb(f"{kind}{side}_hi", [P, G, n], BF16),
                                     sb(f"{kind}{side}_lo", [P, G, n], BF16),
                                     sb(f"{kind}{side}_slots", [P, RH, G, n], BF16))
        v_aug = {"s": sb("v_aug_s", [S, G, UNITS, RH, VW]), "c": sb("v_aug_c", [SK, G, UNITS, RH, VW])}
        neg_max = sb("neg_max", [P, 2, NH])
        nm_parts = sb("nm_parts", [P, P], BF16)
        max_t = sb("max_t", [P, 2, P], BF16)
        probs = sb("probs", [P, 2, RH * S])
        av_sb = sb("av_sb", [P, 2, 2 * S])
        rden = sb("rden", [P, 2, NH])
        att = sb("att", [P, 2, D])
        att_t = sb("att_t", [P, 2, S])
        x_post = sb("x_post", [P, 2, D])
        st6 = sb("st6", [P, 2, 6])
        mv = sb("mv", [P, 2, 2])
        var_e = sb("var_e", [P, 2, 1])
        rstd = sb("rstd", [P, 2, 1])
        y_n = sb("y_n", [P, 2, D])
        y_g = sb("y_g", [P, D])
        x1_t = sb("x1_t", [P, G, S])
        x2_t = sb("x2_t", [P, G, S])
        hid = sb("hid", [P, NF, G, S])
        x3 = sb("x3", [P, G, D])
        st6_f = sb("st6_f", [P, G, 6])
        mv_f = sb("mv_f", [P, G, 2])
        var_f = sb("var_f", [P, G])
        rstd_f = sb("rstd_f", [P, G])
        y3 = sb("y3", [P, G, D])
        y3_g = sb("y3_g", [P, G, D])
        x3_t = sb("x3_t", [P, G, S])
        e_q = sb("e_q", [P, G, S])
        phi_q = sb("phi_q", [P, G, S])
        e_k = sb("e_k", [SK, G, D])
        phi_k = sb("phi_k", [SK, G, D])
        kv_sb = sb("kv_sb", [P, G, D + 1])
        den = sb("den", [P, G])
        rec4 = sb("rec4", [P, G])
        x4 = sb("x4", [P, G, D])
        st6_l = sb("st6_l", [P, G, 6])
        mv_l = sb("mv_l", [P, G, 2])
        var_l = sb("var_l", [P, G])
        rstd_l = sb("rstd_l", [P, G])
        y4 = sb("y4", [P, G, D])
        y4_g = sb("y4_g", [P, G, D])

        s1_ps = [psum(f"s1_ps{n}", [P, RH * S]) for n in range(2)]
        s2_ps = [psum(f"s2_ps{n}", [P, RH * S]) for n in range(2)]
        av_ps = psum("av_ps", [P, 2 * S])
        post_ps = [psum(f"post_ps{n}", [P, 4, S]) for n in range(2)]
        proj_ps = psum("proj_ps", [P, RH * S])

        names = """w_first w_rest cols_in rows_in ident_in mask_in xall_in xt_loaded ct_loaded cn_loaded
            slots_s slots_c stored
            id_set keep_set bias_set sel_set zeros_set any_counted any_set half_set r0_ready resb_set
            s1_ready max_done nm_hi nm_ready nmt_ready maxt_ready s2_ready exp_done av_ready av_copied
            pvt_ready rden_ready att_ready attt_ps attt_ready o_ready xpost_ready st_ready mv_ready var_ready
            rstd_ready yn_ready yt_ready xt_ready yg_ready res_ready
            proj_full proj_read
            hi_sq hi_sk hi_cq hi_ck lo_sq lo_sk lo_cq lo_ck
            st3_ready mv3_ready var3_ready rstd3_ready y3_ready y3g_ready r3_ready
            minq_ready expq_ready phiq_ready mink_ready expk_ready phik_ready
            den_ready rec4_ready st4_ready mv4_ready var4_ready rstd4_ready y4_ready y4g_ready out_ready"""
        M = {n: sem(n) for n in names.split()}

        nmt_ps = s1_ps[1][:, 0:P // 2].bitcast(BF16)

        def wait_full(eng, i, name):
            eng.wait_ge(M["proj_full"], use_index(i, name) + 1)

        def wait_read(eng, i, name):
            eng.wait_ge(M["proj_read"], use_index(i, name) + 1)

        block = ctx.enter_context(nc.Block())

        @block.sync
        def _(sp):
            def load_xt(g):
                sp.dma_start(xt_in[:], x_t[bass.ds(g, 1)].rearrange("a p b n -> (a p) b n")).then_inc(
                    M["xt_loaded"], 16)

            def lay_slots(kind, g, laid):
                for side in "qk":
                    for s in range(4):
                        part = 1 + (s // 2 if side == "q" else s % 2)
                        for r in range(RH):
                            sp.dma_start(split[kind, side][3][s:P:4, r, :, :],
                                         split[kind, side][part][32 * r:32 * r + 32, :, :]).then_inc(laid, 16)

            def settle():
                sp.nop(nofuse=True)

            load_xt(0)
            sp.dma_start(w_sb[:, 0:3, :], weights[:, 0:3, :]).then_inc(M["w_first"], 16)
            sp.dma_start(w_sb[:, 3:N_W, :], weights[:, 3:N_W, :]).then_inc(M["w_rest"], 16)

            def iteration(i):
                if on(i, NEXT) and (not static(i) or i > NEXT):
                    wait_full(sp, i - 1, "sv")
                    settle()
                    load_xt(i - NEXT)
                if on(i, TAIL):
                    wait_reuse(sp, M["phik_ready"], i - TAIL)
                    settle()
                    if not static(i) or i > TAIL:
                        wait_read(sp, i - 1, "kv")
                    settle()
                    sp.dma_start(cn_in[:, :, 0:D], ctx_n[bass.ds((i - TAIL) * G, G)].rearrange(
                        "b k d -> k b d")).then_inc(M["cn_loaded"], 16)
                if on(i, SELF):
                    if on(i, CROSS):
                        wait_full(sp, i, "cv")
                    settle()
                    sp.dma_start(ct_in[:], ctx_t[bass.ds(i, 1)].rearrange("a p b n -> (a p) b n")).then_inc(
                        M["ct_loaded"], 16)
                if on(i, NEXT):
                    g = i - NEXT
                    for part in ("hi_sq", "hi_sk", "lo_sq", "lo_sk"):
                        sp.wait_ge(M[part], g + 1)
                    settle()
                    wait_reuse(sp, M["s2_ready"], UNITS * job_index(i, 2))
                    lay_slots("s", g, M["slots_s"])
                if on(i, SELF):
                    for part in ("hi_cq", "hi_ck", "lo_cq", "lo_ck"):
                        sp.wait_ge(M[part], i + 1)
                    settle()
                    wait_reuse(sp, M["s2_ready"], UNITS * job_index(i, 4))
                    lay_slots("c", i, M["slots_c"])
                if on(i, TAIL):
                    g = i - TAIL
                    sp.wait_ge(M["out_ready"], g + 1)
                    settle()
                    sp.dma_start(out[bass.ds(g * G, G)].rearrange("b p d -> p b d"),
                                 o_all[:, bass.ds(g * G, G), :]).then_inc(M["stored"], 16)

            run_iterations(sp, iteration)
            sp.wait_ge(M["stored"], 16 * NG)

        @block.tensor
        def _(pe):
            pe.wait_ge(M["keep_set"], 1)
            nc.tensor.matmul(post_ps[0][:, 0, :], ones_b[:], keep_k[:], start=True, stop=True).then_inc(
                M["any_counted"], 1)
            pe.wait_ge(M["any_set"], 1)
            pe.wait_ge(M["w_first"], 16)

            def query_major(kind, b, g, job, u):
                n = KLEN[kind]
                q, k = split[kind, "q"][3], split[kind, "k"][3]
                if u == 0 and b == 0:
                    pe.wait_ge(M["slots_" + kind], SLOT_DMAS * 16 * (g + 1))
                wait_reuse(pe, M["max_done"], job * UNITS + u - 1)
                if u == 1:
                    wait_reuse(pe, M["maxt_ready"], job)
                bank = s1_ps[u % 2]
                if kind == "s":
                    nc.tensor.matmul(bank[:, :], id_b[:], bias_q[:].unsqueeze(1).to_broadcast([P, RH, n]),
                                     start=True, stop=False, skip_group_check=True)
                for r in range(RH):
                    last = nc.tensor.matmul(bank[:, r * n:(r + 1) * n], q[32 * u:32 * u + 32, r, b, :],
                                            k[32 * u:32 * u + 32, r, b, :], start=(kind == "c"), stop=True,
                                            skip_group_check=True)
                last.then_inc(M["s1_ready"], 1)

            def transpose_max(job):
                pe.wait_ge(M["nm_ready"], job + 1)
                nc.tensor.transpose(nmt_ps, nm_parts[:], id_b[:]).then_inc(M["nmt_ready"], 1)

            def key_major(kind, b, g, job, u):
                n = KLEN[kind]
                q, k = split[kind, "q"][3], split[kind, "k"][3]
                if u == 0:
                    pe.wait_ge(M["maxt_ready"], job + 1)
                wait_reuse(pe, M["exp_done"], job * UNITS + u - 1)
                bank = s2_ps[u % 2]
                if kind == "s":
                    nc.tensor.matmul(bank[:, :], id_b[:], bias_k[:].unsqueeze(1).to_broadcast([P, RH, S]),
                                     start=True, stop=False, skip_group_check=True)
                for r in range(RH):
                    nc.tensor.matmul(bank[0:n, r * S:(r + 1) * S], head_sel[:, RH * r + u, 0:n], max_t[:, b, :],
                                     start=(kind == "c" and r == 0), stop=False, skip_group_check=True)
                for r in range(RH):
                    last = nc.tensor.matmul(bank[0:n, r * S:(r + 1) * S], k[32 * u:32 * u + 32, r, b, :],
                                            q[32 * u:32 * u + 32, r, b, :], start=False, stop=True,
                                            skip_group_check=True)
                last.then_inc(M["s2_ready"], 1)

            def times_v(i, kind, b, g, job, u):
                if u == 0:
                    wait_reuse(pe, M["av_copied"], job)
                    if b == 0:
                        wait_read(pe, i if kind == "c" else i - 1, kind + "v")
                pe.wait_ge(M["exp_done"], job * UNITS + u + 1)
                rr, a = u // 2, u % 2
                for r in range(RH):
                    last = nc.tensor.matmul(av_ps[32 * r:32 * r + VW, rr * S:(rr + 1) * S],
                                            v_aug[kind][:, b, u, r, :], probs[0:KLEN[kind], u % 2, r * S:(r + 1) * S],
                                            start=(a == 0), stop=(a == 1), skip_group_check=True)
                last.then_inc(M["av_ready"], 1)

            def post_transpose_pv(kind, b, g, job):
                pe.wait_ge(M["av_copied"], job + 1)
                wait_reuse(pe, M["xt_ready"], job - 1)
                for rr in range(2):
                    last = nc.tensor.transpose(post_ps[b][:, rr, :], av_sb[:, b, rr * S:(rr + 1) * S], id_f[:])
                last.then_inc(M["pvt_ready"], 1)

            def post_transpose_att(kind, b, g, job):
                pe.wait_ge(M["att_ready"], job + 1)
                nc.tensor.transpose(post_ps[b][:, 2, :], att[:, b, :], id_f[:]).then_inc(M["attt_ps"], 1)

            def post_project(kind, b, g, job):
                pe.wait_ge(M["attt_ready"], job + 1)
                nc.tensor.matmul(post_ps[b][:, 3, :], att_t[:, b, :], w_sb[:, W_SO if kind == "s" else W_CO, :],
                                 start=True, stop=True).then_inc(M["o_ready"], 1)

            def post_transpose_y(kind, b, g, job):
                pe.wait_ge(M["yn_ready"], job + 1)
                nc.tensor.transpose(post_ps[b][:, 2, :], y_n[:, b, :], id_f[:]).then_inc(M["yt_ready"], 1)

            def open_bank(i, name):
                wait_reuse(pe, M["proj_read"], use_index(i, name))

            def project_t(w, src, at, n):
                return nc.tensor.matmul(proj_ps[:, at:at + n], w_sb[:, w, :], src, start=True, stop=True)

            def project_v(i, name, w, src, n):
                open_bank(i, name)
                for b in range(G):
                    last = nc.tensor.matmul(proj_ps[0:n, b * D:(b + 1) * D], src[:, b, :], w_sb[:, w, :],
                                            start=True, stop=True)
                last.then_inc(M["proj_full"], 1)

            def mlp_up(i, name, c):
                open_bank(i, name)
                project_t(W_1 + c, x2_t[:], 0, G * S)
                project_t(W_1 + c + 1, x2_t[:], G * S, G * S).then_inc(M["proj_full"], 1)

            def mlp_down(i):
                wait_read(pe, i, "h23")
                for b in range(G):
                    for c in range(NF):
                        last = nc.tensor.matmul(proj_ps[:, b * D:(b + 1) * D], hid[:, c, b, :],
                                                w_sb[:, W_2 + c, :], start=(c == 0), stop=(c == NF - 1))
                last.then_inc(M["proj_full"], 1)

            def context_kv(i):
                open_bank(i, "kv")
                for b in range(G):
                    last = nc.tensor.matmul(proj_ps[:, b * (D + 1):(b + 1) * (D + 1)], phi_k[:, b, :], cn_in[:, b, :],
                                            start=True, stop=True)
                last.then_inc(M["proj_full"], 1)

            def transpose_y3(i):
                pe.wait_ge(M["y3_ready"], i - TAIL + 1)
                open_bank(i, "yt")
                for b in range(G):
                    last = nc.tensor.transpose(proj_ps[:, b * S:(b + 1) * S], y3[:, b, :], id_f[:])
                last.then_inc(M["proj_full"], 1)

            def linear_attention(i):
                open_bank(i, "la")
                for b in range(G):
                    last = nc.tensor.matmul(proj_ps[:, b * (D + 1):(b + 1) * (D + 1)], phi_q[:, b, :], kv_sb[:, b, :],
                                            start=True, stop=True)
                last.then_inc(M["proj_full"], 1)

            def light_work(i, k, step):
                if (k, step) == (0, 0) and on(i, CROSS):
                    project_v(i, "cv", W_CV, ct_in, SK)
                if (k, step) == (1, 1) and on(i, TAIL):
                    pe.wait_ge(M["xt_ready"], job_index(i, 0))
                    mlp_up(i, "h01", 0)
                if (k, step) == (1, 2) and on(i, TAIL):
                    mlp_up(i, "h23", 2)
                if (k, step) == (1, 3) and on(i, TAIL):
                    mlp_down(i)
                if (k, step) == (2, 0) and on(i, NEXT):
                    pe.wait_ge(M["xt_loaded"], 16 * (i - NEXT + 1))
                    open_bank(i, "sqk")
                    project_t(W_SQ, xt_in[:], 0, G * S)
                    project_t(W_SK, xt_in[:], G * S, G * S).then_inc(M["proj_full"], 1)
                if (k, step) == (2, 1) and on(i, NEXT):
                    project_v(i, "sv", W_SV, xt_in, S)
                if (k, step) == (2, 2) and on(i, TAIL):
                    pe.wait_ge(M["phik_ready"], i - TAIL + 1)
                    context_kv(i)
                if (k, step) == (2, 3) and on(i, TAIL):
                    transpose_y3(i)
                if (k, step) == (3, 1) and on(i, SELF):
                    pe.wait_ge(M["ct_loaded"], 16 * (i + 1))
                    pe.wait_ge(M["xt_ready"], job_index(i, 2))
                    open_bank(i, "cqk")
                    project_t(W_CQ, x1_t[:], 0, G * S)
                    project_t(W_CK, ct_in[:], G * S, G * SK).then_inc(M["proj_full"], 1)
                if (k, step) == (3, 3) and on(i, TAIL):
                    pe.wait_ge(M["phiq_ready"], i - TAIL + 1)
                    linear_attention(i)

            def iteration(i):
                if static(i) and i == SELF:
                    pe.wait_ge(M["w_rest"], 16)
                for k in range(4):
                    cur, nxt, prev, prev_y = schedule(i, k)
                    for u in range(UNITS):
                        if nxt:
                            if u == 0 and static(i) and i == NEXT:
                                pe.wait_ge(M["bias_set"], 1)
                                pe.wait_ge(M["sel_set"], 1)
                            query_major(*nxt, u)
                        if cur:
                            key_major(*cur, u)
                            if u > 0:
                                times_v(i, *cur, u - 1)
                        if u == 1 and prev_y:
                            post_transpose_y(*prev_y)
                        if u == 1 and prev:
                            post_transpose_pv(*prev)
                        if u == 2 and prev:
                            post_transpose_att(*prev)
                        if u == 3 and prev:
                            post_project(*prev)
                        if u > 0:
                            light_work(i, k, u - 1)
                    if cur:
                        times_v(i, *cur, UNITS - 1)
                    light_work(i, k, 3)
                    if nxt:
                        transpose_max(nxt[3])

            run_iterations(pe, iteration)

        @block.scalar
        def _(act):
            act.dma_start(mask_k_i[:], mask_k).then_inc(M["mask_in"], 16)
            act.dma_start(id_f[:], ident).then_inc(M["ident_in"], 16)
            act.dma_start(col_sb[:], cols).then_inc(M["cols_in"], 16)
            act.dma_start(mask_q_i[:], mask_q).then_inc(M["mask_in"], 16)
            act.dma_start(row_sb[:], rows.unsqueeze(0).to_broadcast([P, N_ROWS, P])).then_inc(M["rows_in"], 16)
            act.dma_start(x_all[:], x.rearrange("b p d -> p b d")).then_inc(M["xall_in"], 16)
            act.wait_ge(M["cols_in"], 16)

            def col(c):
                return col_sb[:, c:c + 1]

            def exp_unit(kind, b, g, job, u):
                n = KLEN[kind]
                act.wait_ge(M["s2_ready"], job * UNITS + u + 1)
                wait_reuse(act, M["av_ready"], job * UNITS + u - 1)
                nc.scalar.activation(probs[0:n, u % 2, :], s2_ps[u % 2][0:n, :], ACT.Exp, scale=SCALE).then_inc(
                    M["exp_done"], 1)

            def copy_max(job, b):
                act.wait_ge(M["nmt_ready"], job + 1)
                wait_reuse(act, M["s2_ready"], (job - 1) * UNITS)
                nc.scalar.copy(max_t[:, b, :], nmt_ps).then_inc(M["maxt_ready"], 1)

            def copy_av(kind, b, g, job):
                act.wait_ge(M["av_ready"], (job + 1) * UNITS)
                wait_reuse(act, M["pvt_ready"], job - 1)
                nc.scalar.copy(av_sb[:, b, :], av_ps[:, :]).then_inc(M["av_copied"], 1)

            def copy_att(kind, b, g, job):
                act.wait_ge(M["attt_ps"], job + 1)
                wait_reuse(act, M["o_ready"], job - 1)
                nc.scalar.copy(att_t[:, b, :], post_ps[b][:, 2, :]).then_inc(M["attt_ready"], 1)

            def scale_y(i, kind, b, g, job):
                dst, gain, bias = (x1_t, C_G1, C_E1) if kind == "s" else (x2_t, C_G2, C_E2)
                act.wait_ge(M["yt_ready"], job + 1)
                if b == 0 and kind == "s" and (not static(i) or i > SELF):
                    wait_full(act, i - 1, "cqk")
                if b == 0 and kind == "c" and (not static(i) or i > TAIL):
                    wait_full(act, i - 1, "h23")
                nc.scalar.activation(dst[:, b, :], post_ps[b][:, 2, :], ACT.Identity, bias=col(bias),
                                     scale=col(gain)).then_inc(M["xt_ready"], 1)

            def split_hi(i, kind, side, g):
                wait_reuse(act, M["slots_" + kind], SLOT_DMAS * 16 * g)
                nc.scalar.copy(split[kind, side][1][:], split[kind, side][0][:]).then_inc(M["hi_" + kind + side], 1)

            def relu(i, name, c):
                wait_full(act, i, name)
                if c == 0 and (not static(i) or i > TAIL):
                    wait_full(act, i - 1, "ff")
                for h in range(2):
                    last = nc.scalar.activation(hid[:, c + h, :, :],
                                                proj_ps[:, h * G * S:(h + 1) * G * S].rearrange("p (b n) -> p b n", b=G),
                                                ACT.Relu, bias=col(C_B1 + c + h))
                last.then_inc(M["proj_read"], 1)

            def light_work(i, k, step):
                if (k, step) == (1, 1) and on(i, TAIL):
                    relu(i, "h01", 0)
                    act.wait_ge(M["mink_ready"], i - TAIL + 1)
                    nc.scalar.activation(e_k[:], e_k[:], ACT.Exp).then_inc(M["expk_ready"], 1)
                if (k, step) == (1, 2) and on(i, TAIL):
                    relu(i, "h23", 2)
                if (k, step) == (2, 0) and on(i, NEXT):
                    wait_read(act, i, "sqk")
                    split_hi(i, "s", "q", i - NEXT)
                    split_hi(i, "s", "k", i - NEXT)
                if (k, step) == (2, 2) and on(i, TAIL):
                    wait_full(act, i, "kv")
                    nc.scalar.copy(kv_sb[:], proj_ps[:, 0:G * (D + 1)].rearrange("p (b n) -> p b n", b=G)).then_inc(
                        M["proj_read"], 1)
                if (k, step) == (2, 3) and on(i, TAIL):
                    wait_full(act, i, "yt")
                    wait_reuse(act, M["phiq_ready"], i - TAIL)
                    nc.scalar.activation(x3_t[:], proj_ps[:, 0:G * S].rearrange("p (b n) -> p b n", b=G), ACT.Identity,
                                         bias=col(C_E3), scale=col(C_G3)).then_inc(M["proj_read"], 1)
                if (k, step) == (3, 1) and on(i, TAIL):
                    act.wait_ge(M["minq_ready"], i - TAIL + 1)
                    nc.scalar.activation(e_q[:], e_q[:], ACT.Exp).then_inc(M["expq_ready"], 1)
                if (k, step) == (3, 1) and on(i, SELF):
                    wait_full(act, i, "cqk")
                    wait_reuse(act, M["lo_cq"], i)
                    wait_reuse(act, M["lo_ck"], i)
                    nc.scalar.activation(split["c", "q"][0][:], proj_ps[:, 0:G * S].rearrange("p (b n) -> p b n", b=G),
                                         ACT.Identity, bias=col(C_CQB))
                    nc.scalar.activation(split["c", "k"][0][:],
                                         proj_ps[:, G * S:G * (S + SK)].rearrange("p (b n) -> p b n", b=G),
                                         ACT.Identity, bias=col(C_CKB)).then_inc(M["proj_read"], 1)
                    wait_read(act, i, "cqk")
                    split_hi(i, "c", "q", i)
                    split_hi(i, "c", "k", i)

            def iteration(i):
                for k in range(4):
                    cur, nxt, prev, prev_y = schedule(i, k)
                    if prev:
                        copy_av(*prev)
                    for u in range(UNITS):
                        if cur:
                            exp_unit(*cur, u)
                        if u == 1 and prev_y:
                            scale_y(i, *prev_y)
                        if u == 2 and prev:
                            copy_att(*prev)
                        if u > 0:
                            light_work(i, k, u - 1)
                    light_work(i, k, 3)
                    if nxt:
                        copy_max(nxt[3], nxt[1])

            run_iterations(act, iteration)

        @block.vector
        def _(dve):
            nc.vector.memset(ones_b[:], 1.0)
            nc.vector.memset(nm_parts[:], 0.0)
            for kind in "sc":
                nc.vector.memset(v_aug[kind][:], 0.0)
            nc.vector.memset(cn_in[:, :, D:D + 1], 1.0).then_inc(M["zeros_set"], 1)
            dve.wait_ge(M["zeros_set"], 1)
            for kind in "sc":
                v = v_aug[kind][:].rearrange("k b (rr a) r w -> k b rr a r w", a=2)
                for b in range(G):
                    for a in range(2):
                        nc.vector.memset(v[:, b, :, a, :, 9 * a + HD:9 * a + HD + 1], 1.0)
            dve.wait_ge(M["mask_in"], 32)
            nc.vector.tensor_scalar(keep_k[:], mask_k_i[:], 0.0, None, ALU.not_equal).then_inc(M["keep_set"], 1)
            nc.vector.tensor_scalar(bias_k[:], mask_k_i[:], 0.0, MASKED, ALU.is_equal, ALU.mult)
            nc.vector.tensor_scalar(bias_q[:], mask_q_i[:], 0.0, MASKED, ALU.is_equal, ALU.mult)
            dve.wait_ge(M["ident_in"], 16)
            nc.vector.tensor_copy(id_b[:], id_f[:]).then_inc(M["bias_set"], 1)
            dve.wait_ge(M["bias_set"], 1)
            nc.vector.tensor_tensor(head_sel[:], id_b[:, 0:NH].unsqueeze(2).to_broadcast([P, NH, P]),
                                    id_b[:, NH:2 * NH].unsqueeze(2).to_broadcast([P, NH, P]), ALU.add).then_inc(
                M["sel_set"], 1)
            dve.wait_ge(M["any_counted"], 1)
            nc.vector.tensor_scalar(any_key[:], post_ps[0][:, 0, :], 0.0, None, ALU.is_gt).then_inc(M["any_set"], 1)
            dve.wait_ge(M["cols_in"], 16)
            dve.wait_ge(M["rows_in"], 16)

            def col(c):
                return col_sb[:, c:c + 1]

            def max_unit(kind, b, g, job, u):
                n = KLEN[kind]
                dve.wait_ge(M["s1_ready"], job * UNITS + u + 1)
                out_ap = neg_max[:, b, :].rearrange("p (r u) -> p r u", u=UNITS)[:, :, u]
                nc.vector.tensor_reduce(out_ap, s1_ps[u % 2][:, 0:RH * n].rearrange("p (r n) -> p r n", r=RH), AX_X,
                                        ALU.max, negate=True).then_inc(M["max_done"], 1)

            def split_max(kind, b, g, job):
                dve.wait_ge(M["max_done"], (job + 1) * UNITS)
                wait_reuse(dve, M["nmt_ready"], job)
                nc.vector.tensor_copy(nm_parts[:, 0:NH], neg_max[:, b, :]).then_inc(M["nm_hi"], 1)
                dve.wait_ge(M["nm_hi"], job + 1)
                nc.vector.tensor_tensor(nm_parts[:, NH:2 * NH], neg_max[:, b, :], nm_parts[:, 0:NH],
                                        ALU.subtract).then_inc(M["nm_ready"], 1)

            def normalise(kind, b, g, job):
                pv = post_ps[b][:, 0:2, :].rearrange("q rr (r w) -> q rr r w", w=VW)
                rd = rden[:, b, :].rearrange("q (a rr r) -> q a rr r", a=2, rr=2)
                dve.wait_ge(M["pvt_ready"], job + 1)
                for a in range(2):
                    last = nc.vector.reciprocal(rd[:, a], pv[:, :, :, 9 * a + HD])
                last.then_inc(M["rden_ready"], 1)
                dve.wait_ge(M["rden_ready"], job + 1)
                wait_reuse(dve, M["attt_ps"], job - 1)
                at = att[:, b, :].rearrange("q (r rr a d) -> q a rr r d", r=RH, rr=2, a=2)
                for a in range(2):
                    last = nc.vector.tensor_tensor(at[:, a], pv[:, :, :, 9 * a:9 * a + HD],
                                                   rd[:, a].unsqueeze(3).to_broadcast([P, 2, RH, HD]), ALU.mult)
                last.then_inc(M["att_ready"], 1)

            def residual(kind, b, g, job):
                res = r0 if kind == "s" else r1
                dve.wait_ge(M["o_ready"], job + 1)
                if kind == "c":
                    dve.wait_ge(M["res_ready"], job - 3)
                nc.vector.tensor_tensor(x_post[:, b, :].unsqueeze(1), post_ps[b][:, 3, :].unsqueeze(1),
                                        res[:, bass.ds(g * G + b, 1), :], ALU.add).then_inc(M["xpost_ready"], 1)
                dve.wait_ge(M["xpost_ready"], job + 1)
                nc.vector.bn_stats(st6[:, b, :], x_post[:, b, :]).then_inc(M["st_ready"], 1)
                dve.wait_ge(M["st_ready"], job + 1)
                dve.nop(nofuse=True)
                nc.vector.bn_aggr(mv[:, b, :], st6[:, b, :]).then_inc(M["mv_ready"], 1)
                dve.wait_ge(M["mv_ready"], job + 1)
                nc.vector.tensor_scalar(var_e[:, b, :], mv[:, b, 1:2], LN_EPS, None, ALU.add).then_inc(
                    M["var_ready"], 1)

            def standardise(kind, b, g, job):
                dve.wait_ge(M["rstd_ready"], job + 1)
                wait_reuse(dve, M["yt_ready"], job - 1)
                wait_reuse(dve, M["yg_ready"], job - 1)
                nc.vector.tensor_scalar(y_n[:, b, :], x_post[:, b, :], mv[:, b, 0:1], rstd[:, b, :], ALU.subtract,
                                        ALU.mult).then_inc(M["yn_ready"], 1)

            def split_lo(kind, side, g):
                f, hi, lo, _ = split[kind, side]
                dve.wait_ge(M["hi_" + kind + side], g + 1)
                wait_reuse(dve, M["slots_" + kind], SLOT_DMAS * 16 * g)
                nc.vector.tensor_tensor(lo[:], f[:], hi[:], ALU.subtract).then_inc(M["lo_" + kind + side], 1)

            def store_v(i, name, kind, bias):
                n = KLEN[kind]
                wait_full(dve, i, name)
                wait_reuse(dve, M["av_ready"], UNITS * job_index(i, 2 if kind == "s" else 0))
                for b in range(G):
                    src = proj_ps[0:n, b * D:(b + 1) * D].rearrange("k (r rr a d) -> k a rr r d", r=RH, rr=2,
                                                                             a=2)
                    vb = row_sb[0:n, bias, :].rearrange("k (r rr a d) -> k a rr r d", r=RH, rr=2, a=2)
                    dst = v_aug[kind][:, b].rearrange("k (rr a) r w -> k a rr r w", a=2)
                    for a in range(2):
                        last = nc.vector.tensor_tensor(dst[:, a, :, :, 9 * a:9 * a + HD], src[:, a], vb[:, a], ALU.add)
                last.then_inc(M["proj_read"], 1)

            def norm_stats(src, st, mom, var, names, g):
                s_st, s_mv, s_var = names
                for b in range(G):
                    last = nc.vector.bn_stats(st[:, b, :], src[:, b, :])
                last.then_inc(M[s_st], 1)
                dve.wait_ge(M[s_st], g + 1)
                dve.nop(nofuse=True)
                for b in range(G):
                    last = nc.vector.bn_aggr(mom[:, b, :], st[:, b, :])
                last.then_inc(M[s_mv], 1)
                dve.wait_ge(M[s_mv], g + 1)
                nc.vector.tensor_scalar(var[:], mom[:, :, 1], LN_EPS, None, ALU.add).then_inc(M[s_var], 1)

            def light_work(i, k, step):
                g = i - TAIL
                if (k, step) == (0, 0) and on(i, CROSS):
                    store_v(i, "cv", "c", R_CVB)
                if (k, step) == (1, 0) and on(i, TAIL):
                    dve.wait_ge(M["cn_loaded"], 16 * (g + 1))
                    nc.vector.tensor_scalar(e_k[:], cn_in[:, :, 0:D], 0.0, None, ALU.min).then_inc(M["mink_ready"], 1)
                if (k, step) == (1, 2) and on(i, TAIL):
                    dve.wait_ge(M["expk_ready"], g + 1)
                    nc.vector.scalar_tensor_tensor(phi_k[:], e_k[:], 1.0, cn_in[:, :, 0:D], ALU.subtract,
                                                   ALU.max).then_inc(M["phik_ready"], 1)
                if (k, step) == (1, 3) and on(i, TAIL):
                    wait_full(dve, i, "ff")
                    dve.wait_ge(M["res_ready"], job_index(i, 0))
                    nc.vector.tensor_tensor(x3[:], proj_ps[:, 0:G * D].rearrange("p (b d) -> p b d", b=G),
                                            r2[:, bass.ds(g * G, G), :], ALU.add).then_inc(M["proj_read"], 1)
                    wait_read(dve, i, "ff")
                    norm_stats(x3, st6_f, mv_f, var_f, ("st3_ready", "mv3_ready", "var3_ready"), g)
                if (k, step) == (2, 0) and on(i, NEXT):
                    wait_full(dve, i, "sqk")
                    nc.vector.scalar_tensor_tensor(split["s", "q"][0][:],
                                                   proj_ps[:, 0:G * S].rearrange("p (b n) -> p b n", b=G), col(C_SQB),
                                                   any_key[:].unsqueeze(1).to_broadcast([P, G, S]), ALU.add, ALU.mult)
                    nc.vector.tensor_scalar(split["s", "k"][0][:],
                                            proj_ps[:, G * S:2 * G * S].rearrange("p (b n) -> p b n", b=G), col(C_SKB),
                                            None, ALU.add).then_inc(M["proj_read"], 1)
                if (k, step) == (2, 1) and on(i, NEXT):
                    split_lo("s", "q", i - NEXT)
                    split_lo("s", "k", i - NEXT)
                    store_v(i, "sv", "s", R_SVB)
                if (k, step) == (2, 1) and on(i, TAIL):
                    dve.wait_ge(M["rstd3_ready"], g + 1)
                    wait_reuse(dve, M["y3g_ready"], g)
                    for b in range(G):
                        last = nc.vector.tensor_scalar(y3[:, b, :], x3[:, b, :], mv_f[:, b, 0:1], rstd_f[:, b:b + 1],
                                                       ALU.subtract, ALU.mult)
                    last.then_inc(M["y3_ready"], 1)
                if (k, step) == (3, 0) and on(i, TAIL):
                    wait_read(dve, i, "yt")
                    nc.vector.tensor_scalar(e_q[:], x3_t[:], 0.0, None, ALU.min).then_inc(M["minq_ready"], 1)
                if (k, step) == (3, 2) and on(i, TAIL):
                    dve.wait_ge(M["expq_ready"], g + 1)
                    nc.vector.scalar_tensor_tensor(phi_q[:], e_q[:], 1.0, x3_t[:], ALU.subtract, ALU.max).then_inc(
                        M["phiq_ready"], 1)
                if (k, step) == (3, 2) and on(i, SELF):
                    split_lo("c", "q", i)
                    split_lo("c", "k", i)
                if (k, step) == (3, 3) and on(i, TAIL):
                    wait_full(dve, i, "la")
                    la = proj_ps[:, 0:G * (D + 1)].rearrange("p (b n) -> p b n", b=G)
                    nc.vector.tensor_scalar(den[:], la[:, :, D], DEN_EPS, None, ALU.add).then_inc(M["den_ready"], 1)
                    dve.wait_ge(M["den_ready"], g + 1)
                    nc.vector.reciprocal(rec4[:], den[:]).then_inc(M["rec4_ready"], 1)
                    dve.wait_ge(M["rec4_ready"], g + 1)
                    dve.wait_ge(M["r3_ready"], g + 1)
                    for b in range(G):
                        last = nc.vector.scalar_tensor_tensor(x4[:, b, :].unsqueeze(1), la[:, b:b + 1, 0:D],
                                                              rec4[:, b:b + 1], r3[:, bass.ds(g * G + b, 1), :],
                                                              ALU.mult, ALU.add)
                    last.then_inc(M["proj_read"], 1)
                    wait_read(dve, i, "la")
                    norm_stats(x4, st6_l, mv_l, var_l, ("st4_ready", "mv4_ready", "var4_ready"), g)
                    dve.wait_ge(M["rstd4_ready"], g + 1)
                    wait_reuse(dve, M["y4g_ready"], g)
                    for b in range(G):
                        last = nc.vector.tensor_scalar(y4[:, b, :], x4[:, b, :], mv_l[:, b, 0:1], rstd_l[:, b:b + 1],
                                                       ALU.subtract, ALU.mult)
                    last.then_inc(M["y4_ready"], 1)

            def iteration(i):
                if static(i) and i == SELF:
                    dve.wait_ge(M["r0_ready"], 1)
                for k in range(4):
                    cur, nxt, prev, prev_y = schedule(i, k)
                    for u in range(UNITS):
                        if nxt:
                            max_unit(*nxt, u)
                            if u == UNITS - 1:
                                split_max(*nxt)
                        if u == 1 and prev:
                            normalise(*prev)
                        if u == 3 and prev:
                            residual(*prev)
                        if u > 0:
                            light_work(i, k, u - 1)
                    if prev:
                        standardise(*prev)
                    light_work(i, k, 3)

            run_iterations(dve, iteration)

        @block.gpsimd
        def _(pool):
            nc.gpsimd.memset(neg_half[:], -0.5).then_inc(M["half_set"], 1)
            pool.wait_ge(M["half_set"], 1)
            pool.wait_ge(M["rows_in"], 16)
            pool.wait_ge(M["xall_in"], 16)

            def row(r, n):
                return row_sb[:, r:r + 1, :].to_broadcast([P, n, P])

            nc.gpsimd.tensor_tensor(r0[:], x_all[:], row(R_SOB, B), ALU.add).then_inc(M["r0_ready"], 1)
            nc.gpsimd.tensor_tensor(res_bias[:, 0, :], row_sb[:, R_E1, :], row_sb[:, R_COB, :], ALU.add)
            nc.gpsimd.tensor_tensor(res_bias[:, 1, :], row_sb[:, R_E2, :], row_sb[:, R_B2, :], ALU.add).then_inc(
                M["resb_set"], 1)
            pool.wait_ge(M["resb_set"], 1)

            def inverse_root(kind, b, g, job):
                pool.wait_ge(M["var_ready"], job + 1)
                nc.gpsimd.tensor_tensor(rstd[:, b, :], var_e[:, b, :], neg_half[:, 0:1], ALU.pow).then_inc(
                    M["rstd_ready"], 1)

            def next_residual(kind, b, g, job):
                gain, n, res = (R_G1, 0, r1) if kind == "s" else (R_G2, 1, r2)
                pool.wait_ge(M["yn_ready"], job + 1)
                nc.gpsimd.tensor_tensor(y_g[:], y_n[:, b, :], row_sb[:, gain, :], ALU.mult).then_inc(M["yg_ready"], 1)
                pool.wait_ge(M["yg_ready"], job + 1)
                nc.gpsimd.tensor_tensor(res[:, bass.ds(g * G + b, 1), :], y_g[:].unsqueeze(1),
                                        res_bias[:, n:n + 1, :], ALU.add).then_inc(M["res_ready"], 1)

            def iteration(i):
                g = i - TAIL
                for k in range(4):
                    cur, nxt, prev, prev_y = schedule(i, k)
                    if k == 2 and on(i, TAIL):
                        pool.wait_ge(M["var3_ready"], g + 1)
                        nc.gpsimd.tensor_tensor(rstd_f[:], var_f[:], neg_half[:], ALU.pow).then_inc(
                            M["rstd3_ready"], 1)
                    if prev:
                        inverse_root(*prev)
                        next_residual(*prev)
                    if k == 2 and on(i, TAIL):
                        pool.wait_ge(M["y3_ready"], g + 1)
                        nc.gpsimd.tensor_tensor(y3_g[:], y3[:], row(R_G3, G), ALU.mult).then_inc(M["y3g_ready"], 1)
                        pool.wait_ge(M["y3g_ready"], g + 1)
                        nc.gpsimd.tensor_tensor(r3[:, bass.ds(g * G, G), :], y3_g[:], row(R_E3, G), ALU.add).then_inc(
                            M["r3_ready"], 1)
                    if k == 3 and on(i, TAIL):
                        pool.wait_ge(M["var4_ready"], g + 1)
                        nc.gpsimd.tensor_tensor(rstd_l[:], var_l[:], neg_half[:], ALU.pow).then_inc(
                            M["rstd4_ready"], 1)
                        pool.wait_ge(M["y4_ready"], g + 1)
                        nc.gpsimd.tensor_tensor(y4_g[:], y4[:], row(R_GAM, G), ALU.mult).then_inc(M["y4g_ready"], 1)
                        pool.wait_ge(M["y4g_ready"], g + 1)
                        nc.gpsimd.tensor_tensor(o_all[:, bass.ds(g * G, G), :], y4_g[:], row(R_BET, G),
                                                ALU.add).then_inc(M["out_ready"], 1)

            run_iterations(pool, iteration)


def kernel(**inputs):
    import numpy as np
    import concourse.bacc as bacc
    from concourse.bass_utils import run_bass_kernel_spmd

    a = {k.replace("L0_xattn_", "").replace("L1_xattn_", ""): np.asarray(v) for k, v in inputs.items()}
    x, c, mask = a["x"], a["ctx_1024"], a["mask_1x1xSxS_ik0"][0, 0]
    b, s, d = x.shape
    sk = c.shape[1]
    square = ["sa_qw", "sa_kw", "sa_vw", "sa_ow", "ca_qw", "ca_kw", "ca_vw", "ca_ow"]
    nf = a["w1"].shape[1] // P
    blocks = [a[n] for n in square] + [a["w1"][:, P * n:P * n + P] for n in range(nf)] + \
             [a["w2"][P * n:P * n + P] for n in range(nf)]
    columns = [a["sa_qb"], a["sa_kb"], a["ca_qb"], a["ca_kb"]] + [a["b1"][P * n:P * n + P] for n in range(nf)] + \
              [a[n] for n in ("g1", "be1", "g2", "be2", "g3", "be3")]
    rows = [a[n] for n in ("sa_vb", "sa_ob", "ca_vb", "ca_ob", "b2", "g1", "be1", "g2", "be2", "g3", "be3", "gamma",
                           "beta")]
    data = {
        "x": x,
        "x_t": x.reshape(b // G, G, s, d).transpose(0, 3, 1, 2),
        "ctx_n": c,
        "ctx_t": c.reshape(b // G, G, sk, d).transpose(0, 3, 1, 2),
        "mask_q": mask,
        "mask_k": mask.T,
        "weights": np.stack(blocks, axis=1),
        "cols": np.stack(columns, axis=1),
        "rows": np.stack(rows),
        "ident": np.eye(P, dtype=np.float32),
    }
    data = {n: np.ascontiguousarray(v) for n, v in data.items()}
    nc = bacc.Bacc("TRN2", target_bir_lowering=False, num_devices=1)
    args = [nc.dram_tensor("in_" + n, v.shape, mybir.dt.from_np(v.dtype), kind="ExternalInput").ap()
            for n, v in data.items()]
    out = nc.dram_tensor("out", (b, s, d), F32, kind="ExternalOutput").ap()
    decoder_layer_kernel(nc, *args, out)
    r = run_bass_kernel_spmd(nc, [{"in_" + n: v for n, v in data.items()}], core_ids=[0])
    return r.results[0]["out"]
```

```python
from contextlib import ExitStack

import concourse.bass as bass
from concourse import mybir

F32 = mybir.dt.float32
BF16 = mybir.dt.bfloat16
I32 = mybir.dt.int32
ALU = mybir.AluOpType
ACT = mybir.ActivationFunctionType
AX_X = mybir.AxisListType.X
AX_XY = mybir.AxisListType.XY

P = 128
NH = 16
HD = 8
UNITS = 4
RH = 4
G = 2
MASKED = -float(2 ** 48)
LN_EPS = 1e-5
DEN_EPS = 1e-6
VW = 32

C_SQB, C_SKB, C_CQB, C_CKB, C_B1, C_G1, C_E1, C_G2, C_E2, C_G3, C_E3 = 0, 1, 2, 3, 4, 8, 9, 10, 11, 12, 13
N_COLS = 14
R_SVB, R_SOB, R_CVB, R_COB, R_B2, R_G1, R_E1, R_G2, R_E2, R_G3, R_E3, R_GAM, R_BET = range(13)
N_ROWS = 13
W_SQ, W_SK, W_SV, W_SO, W_CQ, W_CK, W_CV, W_CO, W_1, W_2 = 0, 1, 2, 3, 4, 5, 6, 7, 8, 12
N_W = 16


def decoder_layer_kernel(nc, x, x_t, ctx_n, ctx_t, mask_q, mask_k, weights, cols, rows, ident, out):
    B, S, D = x.shape
    SK = ctx_n.shape[1]
    NG = B // G
    NF = 4
    SCALE = 1.0 / float(HD) ** 0.5
    KLEN = {"s": S, "c": SK}

    NEXT, SELF, CROSS, TAIL = -1, 0, 1, 2

    def static(i):
        return isinstance(i, int)

    def on(i, first):
        return 0 <= i - first < NG if static(i) else True

    def begun(i, first):
        return min(max(i - first, 0), NG) if static(i) else i - first

    def count(i, firsts, at):
        if static(i):
            return sum(begun(i, f) for f in firsts) + sum(int(on(i, f)) for f in firsts[:at])
        return i * len(firsts) + (at - sum(firsts))

    JOB_STAGES = [SELF, SELF, CROSS, CROSS]

    def job_index(i, k):
        return count(i, JOB_STAGES, k)

    def schedule(i, k):
        def job(at, back=0):
            if at >= 4:
                return job(at - 4, back - 1)
            if at < 0:
                return job(at + 4, back + 1)
            first = JOB_STAGES[at]
            if not on(i - back, first):
                return None
            return ("s" if first == SELF else "c", at % 2, i - back - first, job_index(i - back, at))
        return job(k), job(k + 1), job(k - 1), job(k - 2)

    PROJ_USES = [("cv", CROSS), ("cq0", CROSS), ("ck0", CROSS), ("sqk", NEXT),
                 ("cq1", CROSS), ("ck1", CROSS), ("h01", TAIL), ("h23", TAIL), ("ff", TAIL),
                 ("sq0", NEXT), ("sk0", NEXT), ("kv", TAIL), ("sv", NEXT), ("yt", TAIL),
                 ("sq1", NEXT), ("sk1", NEXT), ("cqk", SELF), ("la", TAIL)]

    PROJ_AT = [(0, 0), (0, 1), (0, 2), (0, 3),
               (1, 0), (1, 1), (1, 2), (1, 3), (1, 4),
               (2, 0), (2, 1), (2, 2), (2, 3), (2, 4),
               (3, 0), (3, 1), (3, 2), (3, 4)]

    def use_index(i, name):
        return count(i, [f for _, f in PROJ_USES], [n for n, _ in PROJ_USES].index(name))

    def wait_reuse(eng, sem, value):
        if not static(value) or value > 0:
            eng.wait_ge(sem, value)

    def run_iterations(eng, iteration):
        for i in range(NEXT, TAIL + 1):
            iteration(i)
        with eng.Fori(TAIL + 1, NG - 1) as i:
            iteration(i)
        for i in range(NG - 1, NG + TAIL):
            iteration(i)

    with ExitStack() as ctx:
        def sb(name, shape, dt=F32):
            return ctx.enter_context(nc.sbuf_tensor(name, shape, dt))

        def psum(name, shape, dt=F32):
            return ctx.enter_context(nc.psum_tensor(name, shape, dt))

        def sem(name):
            return ctx.enter_context(nc.semaphore(name))

        w_sb = sb("w_sb", [P, N_W, P])
        col_sb = sb("col_sb", [P, N_COLS])
        row_sb = sb("row_sb", [P, N_ROWS, P])
        id_f = sb("id_f", [P, P])
        id_b = sb("id_b", [P, P], BF16)
        spread = {(side, part): sb(f"spread_{side}_{part}", [P, UNITS, 4, 32], BF16)
                  for side in "qk" for part in ("hi", "lo")}
        row_is_j = sb("row_is_j", [P, RH])
        max_is_j = sb("max_is_j", [P, RH])
        max_is_u = sb("max_is_u", [P, UNITS])
        unit_sel = sb("unit_sel", [P, UNITS, P], BF16)
        mask_q_i = sb("mask_q_i", [P, S], I32)
        mask_k_i = sb("mask_k_i", [P, S], I32)
        bias_q = sb("bias_q", [P, S], BF16)
        bias_k = sb("bias_k", [P, S], BF16)
        neg_half = sb("neg_half", [P, G])
        res_bias = sb("res_bias", [P, 2, P])
        x_all = sb("x_all", [P, B, D])
        r0 = sb("r0", [P, B, D])
        r1 = sb("r1", [P, B, D])
        r2 = sb("r2", [P, B, D])
        r3 = sb("r3", [P, B, D])
        o_all = sb("o_all", [P, B, D])
        xt_in = sb("xt_in", [P, G, S])
        ct_in = sb("ct_in", [P, G, SK])
        cn_in = sb("cn_in", [SK, G, D + 1])
        hi, lo, rows_qk, wide = {}, {}, {}, {}
        for kind in "sc":
            for side in "qk":
                n = KLEN[kind] if side == "k" else S
                key = kind + side
                hi[key] = sb(f"{key}_hi", [P, G, n], BF16)
                lo[key] = sb(f"{key}_lo", [P, G, n], BF16)
                rows_qk[key] = sb(f"{key}_rows", [P, G, UNITS, n], BF16)
                wide[key] = sb(f"{key}_wide", [P, G, RH, UNITS, n], BF16)
        v_aug = {"s": sb("v_aug_s", [S, G, UNITS, RH, VW]), "c": sb("v_aug_c", [SK, G, UNITS, RH, VW])}
        neg_max = sb("neg_max", [P, 2, NH])
        nm_parts = sb("nm_parts", [P, P], BF16)
        max_x = sb("max_x", [P, 2, RH, S], BF16)
        probs = sb("probs", [P, 2, RH * S])
        av_sb = sb("av_sb", [P, 2, 2 * S])
        rden = sb("rden", [P, 2, NH])
        att = sb("att", [P, 2, D])
        att_t = sb("att_t", [P, 2, S])
        x_post = sb("x_post", [P, 2, D])
        st6 = sb("st6", [P, 2, 6])
        mv = sb("mv", [P, 2, 2])
        var_e = sb("var_e", [P, 2, 1])
        rstd = sb("rstd", [P, 2, 1])
        y_n = sb("y_n", [P, 2, D])
        y_g = sb("y_g", [P, D])
        x1_t = sb("x1_t", [P, G, S])
        x2_t = sb("x2_t", [P, G, S])
        hid = sb("hid", [P, NF, G, S])
        x3 = sb("x3", [P, G, D])
        st6_f = sb("st6_f", [P, G, 6])
        mv_f = sb("mv_f", [P, G, 2])
        var_f = sb("var_f", [P, G])
        rstd_f = sb("rstd_f", [P, G])
        y3 = sb("y3", [P, G, D])
        y3_g = sb("y3_g", [P, G, D])
        x3_t = sb("x3_t", [P, G, S])
        e_q = sb("e_q", [P, G, S])
        phi_q = sb("phi_q", [P, G, S])
        e_k = sb("e_k", [SK, G, D])
        phi_k = sb("phi_k", [SK, G, D])
        kv_sb = sb("kv_sb", [P, G, D + 1])
        den = sb("den", [P, G])
        rec4 = sb("rec4", [P, G])
        x4 = sb("x4", [P, G, D])
        st6_l = sb("st6_l", [P, G, 6])
        mv_l = sb("mv_l", [P, G, 2])
        var_l = sb("var_l", [P, G])
        rstd_l = sb("rstd_l", [P, G])
        y4 = sb("y4", [P, G, D])
        y4_g = sb("y4_g", [P, G, D])

        s1_ps = [psum(f"s1_ps{n}", [P, RH * S]) for n in range(2)]
        s2_ps = [psum(f"s2_ps{n}", [P, RH * S]) for n in range(2)]
        av_ps = psum("av_ps", [P, 2 * S])
        post_ps = [psum(f"post_ps{n}", [P, 4, S]) for n in range(2)]
        proj_ps = psum("proj_ps", [P, RH * S])

        names = """w_first w_rest cols_in rows_in ident_in mask_in xall_in xt_loaded ct_loaded cn_loaded
            stored
            id_set bias_set spread_set masks_set unit_set zeros_set half_set r0_ready resb_set
            s1_ready max_done nm_hi nm_ready nmt_ready maxt_ready s2_ready exp_done av_ready av_copied
            pvt_ready rden_ready att_ready attt_ps attt_ready o_ready xpost_ready st_ready mv_ready var_ready
            rstd_ready yn_ready yt_ready xt_ready yg_ready res_ready
            proj_full proj_read
            hi_sqk hi_cqk wide_sq wide_sk wide_cq wide_ck
            st3_ready mv3_ready var3_ready rstd3_ready y3_ready y3g_ready r3_ready
            minq_ready expq_ready phiq_ready mink_ready expk_ready phik_ready
            den_ready rec4_ready st4_ready mv4_ready var4_ready rstd4_ready y4_ready y4g_ready out_ready"""
        M = {n: sem(n) for n in names.split()}

        nmt_ps = s1_ps[1][:, 0:P // 2].bitcast(BF16)

        def wait_full(eng, i, name):
            eng.wait_ge(M["proj_full"], use_index(i, name) + 1)

        def wait_read(eng, i, name):
            eng.wait_ge(M["proj_read"], use_index(i, name) + 1)

        block = ctx.enter_context(nc.Block())

        def wait_rows(eng, kind, side, b, g):
            wait_read(eng, g + (NEXT if kind == "s" else CROSS), kind + side + str(b))

        @block.sync
        def _(sp):
            def load_xt(g):
                sp.dma_start(xt_in[:], x_t[bass.ds(g, 1)].rearrange("a p b n -> (a p) b n")).then_inc(
                    M["xt_loaded"], 16)

            def settle():
                sp.nop(nofuse=True)

            load_xt(0)
            sp.dma_start(w_sb[:, 0:3, :], weights[:, 0:3, :]).then_inc(M["w_first"], 16)
            sp.dma_start(w_sb[:, 3:N_W, :], weights[:, 3:N_W, :]).then_inc(M["w_rest"], 16)

            def iteration(i):
                if on(i, NEXT) and (not static(i) or i > NEXT):
                    wait_full(sp, i - 1, "sv")
                    settle()
                    load_xt(i - NEXT)
                if on(i, TAIL):
                    wait_reuse(sp, M["phik_ready"], i - TAIL)
                    settle()
                    if not static(i) or i > TAIL:
                        wait_read(sp, i - 1, "kv")
                    settle()
                    sp.dma_start(cn_in[:, :, 0:D], ctx_n[bass.ds((i - TAIL) * G, G)].rearrange(
                        "b k d -> k b d")).then_inc(M["cn_loaded"], 16)
                if on(i, SELF):
                    if on(i, CROSS):
                        wait_full(sp, i, "cv")
                    settle()
                    sp.dma_start(ct_in[:], ctx_t[bass.ds(i, 1)].rearrange("a p b n -> (a p) b n")).then_inc(
                        M["ct_loaded"], 16)
                if on(i, TAIL):
                    g = i - TAIL
                    sp.wait_ge(M["out_ready"], g + 1)
                    settle()
                    sp.dma_start(out[bass.ds(g * G, G)].rearrange("b p d -> p b d"),
                                 o_all[:, bass.ds(g * G, G), :]).then_inc(M["stored"], 16)

            run_iterations(sp, iteration)
            sp.wait_ge(M["stored"], 16 * NG)

        @block.tensor
        def _(pe):
            pe.wait_ge(M["w_first"], 16)

            def query_major(kind, b, g, job, u):
                n = KLEN[kind]
                if u == 0:
                    wait_rows(pe, kind, "q", b, g)
                    pe.wait_ge(M[f"wide_{kind}k"], G * g + b + 1)
                wait_reuse(pe, M["max_done"], job * UNITS + u - 1)
                if u == 1:
                    wait_reuse(pe, M["maxt_ready"], job)
                bank = s1_ps[u % 2]
                if kind == "s":
                    nc.tensor.matmul(bank[:, :], id_b[:], bias_q[:].unsqueeze(1).to_broadcast([P, RH, n]),
                                     start=True, stop=False)
                nc.tensor.matmul(bank[:, 0:RH * n], rows_qk[kind + "q"][:, b, u, :], wide[kind + "k"][:, b, :, u, :],
                                 start=(kind == "c"), stop=True).then_inc(M["s1_ready"], 1)

            def transpose_max(job):
                pe.wait_ge(M["nm_ready"], job + 1)
                nc.tensor.transpose(nmt_ps, nm_parts[:], id_b[:]).then_inc(M["nmt_ready"], 1)

            def key_major(kind, b, g, job, u):
                n = KLEN[kind]
                if u == 0:
                    wait_rows(pe, kind, "k", b, g)
                    pe.wait_ge(M[f"wide_{kind}q"], G * g + b + 1)
                wait_reuse(pe, M["exp_done"], job * UNITS + u - 1)
                bank = s2_ps[u % 2]
                if kind == "s":
                    nc.tensor.matmul(bank[:, :], id_b[:], bias_k[:].unsqueeze(1).to_broadcast([P, RH, S]),
                                     start=True, stop=False)
                nc.tensor.matmul(bank[0:n, :], rows_qk[kind + "k"][:, b, u, :], wide[kind + "q"][:, b, :, u, :],
                                 start=(kind == "c"), stop=False)
                if u == 0:
                    pe.wait_ge(M["maxt_ready"], job + 1)
                nc.tensor.matmul(bank[0:n, :], unit_sel[:, u, 0:n], max_x[:, b, :, :], start=False,
                                 stop=True).then_inc(M["s2_ready"], 1)

            def times_v(i, kind, b, g, job, u):
                if u == 0:
                    wait_reuse(pe, M["av_copied"], job)
                    if b == 0:
                        wait_read(pe, i if kind == "c" else i - 1, kind + "v")
                pe.wait_ge(M["exp_done"], job * UNITS + u + 1)
                rr, a = u // 2, u % 2
                for r in range(RH):
                    last = nc.tensor.matmul(av_ps[32 * r:32 * r + VW, rr * S:(rr + 1) * S],
                                            v_aug[kind][:, b, u, r, :], probs[0:KLEN[kind], u % 2, r * S:(r + 1) * S],
                                            start=(a == 0), stop=(a == 1), skip_group_check=True)
                last.then_inc(M["av_ready"], 1)

            def post_transpose_pv(kind, b, g, job):
                pe.wait_ge(M["av_copied"], job + 1)
                wait_reuse(pe, M["xt_ready"], job - 1)
                for rr in range(2):
                    last = nc.tensor.transpose(post_ps[b][:, rr, :], av_sb[:, b, rr * S:(rr + 1) * S], id_f[:])
                last.then_inc(M["pvt_ready"], 1)

            def post_transpose_att(kind, b, g, job):
                pe.wait_ge(M["att_ready"], job + 1)
                nc.tensor.transpose(post_ps[b][:, 2, :], att[:, b, :], id_f[:]).then_inc(M["attt_ps"], 1)

            def post_project(kind, b, g, job):
                pe.wait_ge(M["attt_ready"], job + 1)
                nc.tensor.matmul(post_ps[b][:, 3, :], att_t[:, b, :], w_sb[:, W_SO if kind == "s" else W_CO, :],
                                 start=True, stop=True).then_inc(M["o_ready"], 1)

            def post_transpose_y(kind, b, g, job):
                pe.wait_ge(M["yn_ready"], job + 1)
                nc.tensor.transpose(post_ps[b][:, 2, :], y_n[:, b, :], id_f[:]).then_inc(M["yt_ready"], 1)

            def open_bank(i, name):
                wait_reuse(pe, M["proj_read"], use_index(i, name))

            def project_t(w, src, at, n):
                return nc.tensor.matmul(proj_ps[:, at:at + n], w_sb[:, w, :], src, start=True, stop=True)

            def project_v(i, name, w, src, n):
                open_bank(i, name)
                for b in range(G):
                    last = nc.tensor.matmul(proj_ps[0:n, b * D:(b + 1) * D], src[:, b, :], w_sb[:, w, :],
                                            start=True, stop=True)
                last.then_inc(M["proj_full"], 1)

            def mlp_up(i, name, c):
                open_bank(i, name)
                project_t(W_1 + c, x2_t[:], 0, G * S)
                project_t(W_1 + c + 1, x2_t[:], G * S, G * S).then_inc(M["proj_full"], 1)

            def mlp_down(i):
                wait_read(pe, i, "h23")
                for b in range(G):
                    for c in range(NF):
                        last = nc.tensor.matmul(proj_ps[:, b * D:(b + 1) * D], hid[:, c, b, :],
                                                w_sb[:, W_2 + c, :], start=(c == 0), stop=(c == NF - 1))
                last.then_inc(M["proj_full"], 1)

            def context_kv(i):
                open_bank(i, "kv")
                for b in range(G):
                    last = nc.tensor.matmul(proj_ps[:, b * (D + 1):(b + 1) * (D + 1)], phi_k[:, b, :], cn_in[:, b, :],
                                            start=True, stop=True)
                last.then_inc(M["proj_full"], 1)

            def transpose_y3(i):
                pe.wait_ge(M["y3_ready"], i - TAIL + 1)
                open_bank(i, "yt")
                for b in range(G):
                    last = nc.tensor.transpose(proj_ps[:, b * S:(b + 1) * S], y3[:, b, :], id_f[:])
                last.then_inc(M["proj_full"], 1)

            def linear_attention(i):
                open_bank(i, "la")
                for b in range(G):
                    last = nc.tensor.matmul(proj_ps[:, b * (D + 1):(b + 1) * (D + 1)], phi_q[:, b, :], kv_sb[:, b, :],
                                            start=True, stop=True)
                last.then_inc(M["proj_full"], 1)

            def spread_rows(i, name):
                kind, side, b = name[0], name[1], int(name[2])
                open_bank(i, name)
                n = KLEN[kind] if side == "k" else S
                for u in range(UNITS):
                    nc.tensor.matmul(proj_ps[:, u * n:(u + 1) * n], spread[side, "hi"][:, u, :, :],
                                     hi[kind + side][:, b, :], start=True, stop=False)
                    last = nc.tensor.matmul(proj_ps[:, u * n:(u + 1) * n], spread[side, "lo"][:, u, :, :],
                                            lo[kind + side][:, b, :], start=False, stop=True)
                last.then_inc(M["proj_full"], 1)

            def light_work(i, k, u):
                for (name, stage), at in zip(PROJ_USES, PROJ_AT):
                    if at == (k, u) and on(i, stage):
                        if name == "cv":
                            project_v(i, "cv", W_CV, ct_in, SK)
                        elif name[1] in "qk" and name[2:] in ("0", "1"):
                            if name[2] == "0":
                                wait_read(pe, i if name[0] == "s" else i - 1, name[0] + "qk")
                            spread_rows(i, name)
                        elif name == "sqk":
                            pe.wait_ge(M["xt_loaded"], 16 * (i - NEXT + 1))
                            open_bank(i, "sqk")
                            project_t(W_SQ, xt_in[:], 0, G * S)
                            project_t(W_SK, xt_in[:], G * S, G * S).then_inc(M["proj_full"], 1)
                        elif name == "h01":
                            pe.wait_ge(M["xt_ready"], job_index(i, 0))
                            mlp_up(i, "h01", 0)
                        elif name == "h23":
                            mlp_up(i, "h23", 2)
                        elif name == "ff":
                            mlp_down(i)
                        elif name == "kv":
                            pe.wait_ge(M["phik_ready"], i - TAIL + 1)
                            context_kv(i)
                        elif name == "sv":
                            project_v(i, "sv", W_SV, xt_in, S)
                        elif name == "yt":
                            transpose_y3(i)
                        elif name == "cqk":
                            pe.wait_ge(M["ct_loaded"], 16 * (i + 1))
                            pe.wait_ge(M["xt_ready"], job_index(i, 2))
                            open_bank(i, "cqk")
                            project_t(W_CQ, x1_t[:], 0, G * S)
                            project_t(W_CK, ct_in[:], G * S, G * SK).then_inc(M["proj_full"], 1)
                        elif name == "la":
                            pe.wait_ge(M["phiq_ready"], i - TAIL + 1)
                            linear_attention(i)

            def iteration(i):
                if static(i) and i == SELF:
                    pe.wait_ge(M["w_rest"], 16)
                if static(i) and i == NEXT:
                    pe.wait_ge(M["spread_set"], 1)
                    pe.wait_ge(M["bias_set"], 1)
                    pe.wait_ge(M["unit_set"], 1)
                for k in range(4):
                    cur, nxt, prev, prev_y = schedule(i, k)
                    for u in range(UNITS):
                        if nxt:
                            query_major(*nxt, u)
                        if cur:
                            key_major(*cur, u)
                        light_work(i, k, u)
                        if cur and u > 0:
                            times_v(i, *cur, u - 1)
                        if u == 1 and prev_y:
                            post_transpose_y(*prev_y)
                        if u == 1 and prev:
                            post_transpose_pv(*prev)
                        if u == 2 and prev:
                            post_transpose_att(*prev)
                        if u == 3 and prev:
                            post_project(*prev)
                    if cur:
                        times_v(i, *cur, UNITS - 1)
                    if nxt:
                        transpose_max(nxt[3])
                    light_work(i, k, UNITS)

            run_iterations(pe, iteration)

        @block.scalar
        def _(act):
            act.dma_start(mask_k_i[:], mask_k).then_inc(M["mask_in"], 16)
            act.dma_start(id_f[:], ident).then_inc(M["ident_in"], 16)
            act.dma_start(col_sb[:], cols).then_inc(M["cols_in"], 16)
            act.dma_start(mask_q_i[:], mask_q).then_inc(M["mask_in"], 16)
            act.dma_start(row_sb[:], rows.unsqueeze(0).to_broadcast([P, N_ROWS, P])).then_inc(M["rows_in"], 16)
            act.dma_start(x_all[:], x.rearrange("b p d -> p b d")).then_inc(M["xall_in"], 16)
            act.wait_ge(M["cols_in"], 16)

            def col(c):
                return col_sb[:, c:c + 1]

            def exp_unit(kind, b, g, job, u):
                n = KLEN[kind]
                act.wait_ge(M["s2_ready"], job * UNITS + u + 1)
                wait_reuse(act, M["av_ready"], job * UNITS + u - 1)
                nc.scalar.activation(probs[0:n, u % 2, :], s2_ps[u % 2][0:n, :], ACT.Exp, scale=SCALE).then_inc(
                    M["exp_done"], 1)

            def copy_av(kind, b, g, job):
                act.wait_ge(M["av_ready"], (job + 1) * UNITS)
                wait_reuse(act, M["pvt_ready"], job - 1)
                nc.scalar.copy(av_sb[:, b, :], av_ps[:, :]).then_inc(M["av_copied"], 1)

            def copy_att(kind, b, g, job):
                act.wait_ge(M["attt_ps"], job + 1)
                wait_reuse(act, M["o_ready"], job - 1)
                nc.scalar.copy(att_t[:, b, :], post_ps[b][:, 2, :]).then_inc(M["attt_ready"], 1)

            def scale_y(i, kind, b, g, job):
                dst, gain, bias = (x1_t, C_G1, C_E1) if kind == "s" else (x2_t, C_G2, C_E2)
                act.wait_ge(M["yt_ready"], job + 1)
                if b == 0 and kind == "s" and (not static(i) or i > SELF):
                    wait_full(act, i - 1, "cqk")
                if b == 0 and kind == "c" and (not static(i) or i > TAIL):
                    wait_full(act, i - 1, "h23")
                nc.scalar.activation(dst[:, b, :], post_ps[b][:, 2, :], ACT.Identity, bias=col(bias),
                                     scale=col(gain)).then_inc(M["xt_ready"], 1)

            def split_hi(i, name, kind):
                wait_full(act, i, name)
                for side, at, c in (("q", 0, C_SQB if kind == "s" else C_CQB), ("k", G * S, C_SKB if kind == "s" else C_CKB)):
                    dst = hi[kind + side]
                    n = dst.shape[2]
                    last = nc.scalar.activation(dst[:], proj_ps[:, at:at + G * n].rearrange("p (b n) -> p b n", b=G),
                                                ACT.Identity, bias=col(c))
                last.then_inc(M["hi_" + name], 1)

            def copy_rows(i, name):
                kind, side, b = name[0], name[1], int(name[2])
                n = KLEN[kind] if side == "k" else S
                wait_full(act, i, name)
                wait_reuse(act, M["s2_ready"], UNITS * job_index(i, b + 1 if kind == "s" else 0))
                g = i - (NEXT if kind == "s" else CROSS)
                wait_reuse(act, M[f"wide_{name[:2]}"], G * (g - 1) + b + 1 if not static(g) or g > 0 else 0)
                nc.scalar.copy(rows_qk[name[:2]][:, b, :, :], proj_ps[:, 0:UNITS * n].rearrange(
                    "p (u n) -> p u n", u=UNITS)).then_inc(M["proj_read"], 1)

            def relu(i, name, c):
                wait_full(act, i, name)
                if c == 0 and (not static(i) or i > TAIL):
                    wait_full(act, i - 1, "ff")
                for h in range(2):
                    last = nc.scalar.activation(hid[:, c + h, :, :],
                                                proj_ps[:, h * G * S:(h + 1) * G * S].rearrange("p (b n) -> p b n", b=G),
                                                ACT.Relu, bias=col(C_B1 + c + h))
                last.then_inc(M["proj_read"], 1)

            def light_work(i, k, u):
                if (k, u) == (1, 0) and on(i, TAIL):
                    act.wait_ge(M["mink_ready"], i - TAIL + 1)
                    nc.scalar.activation(e_k[:], e_k[:], ACT.Exp).then_inc(M["expk_ready"], 1)
                if (k, u) == (3, 0) and on(i, TAIL):
                    act.wait_ge(M["minq_ready"], i - TAIL + 1)
                    nc.scalar.activation(e_q[:], e_q[:], ACT.Exp).then_inc(M["expq_ready"], 1)
                for (name, stage), at in zip(PROJ_USES, PROJ_AT):
                    if at == (k, u) and on(i, stage):
                        if name in ("sqk", "cqk"):
                            split_hi(i, name, name[0])
                        elif name[1] in "qk" and name[2:] in ("0", "1"):
                            copy_rows(i, name)
                        elif name == "h01":
                            relu(i, name, 0)
                        elif name == "h23":
                            relu(i, name, 2)
                        elif name == "kv":
                            wait_full(act, i, "kv")
                            nc.scalar.copy(kv_sb[:], proj_ps[:, 0:G * (D + 1)].rearrange(
                                "p (b n) -> p b n", b=G)).then_inc(M["proj_read"], 1)
                        elif name == "yt":
                            wait_full(act, i, "yt")
                            wait_reuse(act, M["phiq_ready"], i - TAIL)
                            nc.scalar.activation(x3_t[:], proj_ps[:, 0:G * S].rearrange("p (b n) -> p b n", b=G),
                                                 ACT.Identity, bias=col(C_E3), scale=col(C_G3)).then_inc(
                                M["proj_read"], 1)

            def iteration(i):
                for k in range(4):
                    cur, nxt, prev, prev_y = schedule(i, k)
                    if prev:
                        copy_av(*prev)
                    for u in range(UNITS):
                        if cur:
                            exp_unit(*cur, u)
                        if u == 2 and prev_y:
                            scale_y(i, *prev_y)
                        light_work(i, k, u)
                        if u == 2 and prev:
                            copy_att(*prev)
                    light_work(i, k, UNITS)

            run_iterations(act, iteration)

        @block.vector
        def _(dve):
            nc.vector.memset(nm_parts[:], 0.0)
            for kind in "sc":
                nc.vector.memset(v_aug[kind][:], 0.0)
            for tile in spread.values():
                nc.vector.memset(tile[:], 0.0)
            nc.vector.memset(cn_in[:, :, D:D + 1], 1.0).then_inc(M["zeros_set"], 1)
            dve.wait_ge(M["zeros_set"], 1)
            for kind in "sc":
                v = v_aug[kind][:].rearrange("k b (rr a) r w -> k b rr a r w", a=2)
                for b in range(G):
                    for a in range(2):
                        nc.vector.memset(v[:, b, :, a, :, 9 * a + HD:9 * a + HD + 1], 1.0)
            dve.wait_ge(M["mask_in"], 32)
            nc.vector.tensor_scalar(bias_k[:], mask_k_i[:], 0.0, MASKED, ALU.is_equal, ALU.mult)
            nc.vector.tensor_scalar(bias_q[:], mask_q_i[:], 0.0, MASKED, ALU.is_equal, ALU.mult)
            dve.wait_ge(M["ident_in"], 16)
            nc.vector.tensor_copy(id_b[:], id_f[:]).then_inc(M["bias_set"], 1)
            dve.wait_ge(M["bias_set"], 1)
            for (side, part), tile in spread.items():
                for s in range(4):
                    if (s // 2 if side == "q" else s % 2) == (part == "lo"):
                        last = nc.vector.tensor_copy(tile[:, :, s, :], id_b[:].rearrange("p (u m) -> p u m", u=UNITS))
            last.then_inc(M["spread_set"], 1)
            by_row = id_f[:].rearrange("p (s j i) -> p j s i", s=4, j=RH)
            by_head = id_f[:, 0:2 * NH].rearrange("p (c u j) -> p c u j", c=2, u=UNITS)
            nc.vector.tensor_reduce(row_is_j[:], by_row, AX_XY, ALU.add)
            nc.vector.tensor_reduce(max_is_j[:], by_head.rearrange("p c u j -> p j c u"), AX_XY, ALU.add)
            nc.vector.tensor_reduce(max_is_u[:], by_head.rearrange("p c u j -> p u c j"), AX_XY, ALU.add).then_inc(
                M["masks_set"], 1)
            dve.wait_ge(M["masks_set"], 1)
            nc.vector.tensor_copy(unit_sel[:], max_is_u[:].unsqueeze(2).to_broadcast([P, UNITS, P])).then_inc(
                M["unit_set"], 1)
            dve.wait_ge(M["cols_in"], 16)
            dve.wait_ge(M["rows_in"], 16)

            def col(c):
                return col_sb[:, c:c + 1]

            def max_unit(kind, b, g, job, u):
                n = KLEN[kind]
                dve.wait_ge(M["s1_ready"], job * UNITS + u + 1)
                nc.vector.tensor_reduce(neg_max[:, b, RH * u:RH * (u + 1)], s1_ps[u % 2][:, 0:RH * n].rearrange("p (r n) -> p r n", r=RH), AX_X,
                                        ALU.max, negate=True).then_inc(M["max_done"], 1)

            def split_max(kind, b, g, job):
                dve.wait_ge(M["max_done"], (job + 1) * UNITS)
                wait_reuse(dve, M["nmt_ready"], job)
                nc.vector.tensor_copy(nm_parts[:, 0:NH], neg_max[:, b, :]).then_inc(M["nm_hi"], 1)
                dve.wait_ge(M["nm_hi"], job + 1)
                nc.vector.tensor_tensor(nm_parts[:, NH:2 * NH], neg_max[:, b, :], nm_parts[:, 0:NH],
                                        ALU.subtract).then_inc(M["nm_ready"], 1)

            def widen_max(kind, b, g, job):
                dve.wait_ge(M["nmt_ready"], job + 1)
                wait_reuse(dve, M["s2_ready"], (job - 1) * UNITS)
                nc.vector.tensor_tensor(max_x[:, b, :, :], nmt_ps.unsqueeze(1).to_broadcast([P, RH, S]),
                                        max_is_j[:].unsqueeze(2).to_broadcast([P, RH, S]), ALU.mult).then_inc(
                    M["maxt_ready"], 1)

            def normalise(kind, b, g, job):
                pv = post_ps[b][:, 0:2, :].rearrange("q rr (r w) -> q rr r w", w=VW)
                rd = rden[:, b, :].rearrange("q (a rr r) -> q a rr r", a=2, rr=2)
                dve.wait_ge(M["pvt_ready"], job + 1)
                for a in range(2):
                    last = nc.vector.reciprocal(rd[:, a], pv[:, :, :, 9 * a + HD])
                last.then_inc(M["rden_ready"], 1)
                dve.wait_ge(M["rden_ready"], job + 1)
                wait_reuse(dve, M["attt_ps"], job - 1)
                at = att[:, b, :].rearrange("q (rr a r d) -> q a rr r d", r=RH, rr=2, a=2)
                for a in range(2):
                    last = nc.vector.tensor_tensor(at[:, a], pv[:, :, :, 9 * a:9 * a + HD],
                                                   rd[:, a].unsqueeze(3).to_broadcast([P, 2, RH, HD]), ALU.mult)
                last.then_inc(M["att_ready"], 1)

            def residual(kind, b, g, job):
                res = r0 if kind == "s" else r1
                dve.wait_ge(M["o_ready"], job + 1)
                if kind == "c":
                    dve.wait_ge(M["res_ready"], job - 3)
                nc.vector.tensor_tensor(x_post[:, b, :].unsqueeze(1), post_ps[b][:, 3, :].unsqueeze(1),
                                        res[:, bass.ds(g * G + b, 1), :], ALU.add).then_inc(M["xpost_ready"], 1)
                dve.wait_ge(M["xpost_ready"], job + 1)
                nc.vector.bn_stats(st6[:, b, :], x_post[:, b, :]).then_inc(M["st_ready"], 1)
                dve.wait_ge(M["st_ready"], job + 1)
                dve.nop(nofuse=True)
                nc.vector.bn_aggr(mv[:, b, :], st6[:, b, :]).then_inc(M["mv_ready"], 1)
                dve.wait_ge(M["mv_ready"], job + 1)
                nc.vector.tensor_scalar(var_e[:, b, :], mv[:, b, 1:2], LN_EPS, None, ALU.add).then_inc(
                    M["var_ready"], 1)

            def standardise(kind, b, g, job):
                dve.wait_ge(M["rstd_ready"], job + 1)
                wait_reuse(dve, M["yt_ready"], job - 1)
                wait_reuse(dve, M["yg_ready"], job - 1)
                nc.vector.tensor_scalar(y_n[:, b, :], x_post[:, b, :], mv[:, b, 0:1], rstd[:, b, :], ALU.subtract,
                                        ALU.mult).then_inc(M["yn_ready"], 1)

            def split_lo(i, name, kind):
                dve.wait_ge(M["hi_" + name], (i - (NEXT if kind == "s" else SELF)) + 1)
                for side, at, c in (("q", 0, C_SQB if kind == "s" else C_CQB), ("k", G * S, C_SKB if kind == "s" else C_CKB)):
                    key = kind + side
                    n = lo[key].shape[2]
                    last = nc.vector.scalar_tensor_tensor(
                        lo[key][:], proj_ps[:, at:at + G * n].rearrange("p (b n) -> p b n", b=G), col(c), hi[key][:],
                        ALU.add, ALU.subtract)
                last.then_inc(M["proj_read"], 1)

            def widen(i, name):
                key, b = name[:2], int(name[2])
                wait_read(dve, i, name)
                for j in range(RH):
                    last = nc.vector.tensor_scalar(wide[key][:, b, j, :, :], rows_qk[key][:, b, :, :],
                                                   row_is_j[:, j:j + 1], None, ALU.mult)
                last.then_inc(M["wide_" + key], 1)

            def store_v(i, name, kind, bias):
                n = KLEN[kind]
                wait_full(dve, i, name)
                wait_reuse(dve, M["av_ready"], UNITS * job_index(i, 2 if kind == "s" else 0))
                for b in range(G):
                    src = proj_ps[0:n, b * D:(b + 1) * D].rearrange("k (rr a r d) -> k a rr r d", r=RH, rr=2, a=2)
                    vb = row_sb[0:n, bias, :].rearrange("k (rr a r d) -> k a rr r d", r=RH, rr=2, a=2)
                    dst = v_aug[kind][:, b].rearrange("k (rr a) r w -> k a rr r w", a=2)
                    for a in range(2):
                        last = nc.vector.tensor_tensor(dst[:, a, :, :, 9 * a:9 * a + HD], src[:, a], vb[:, a], ALU.add)
                last.then_inc(M["proj_read"], 1)

            def norm_stats(src, st, mom, var, names, g):
                s_st, s_mv, s_var = names
                for b in range(G):
                    last = nc.vector.bn_stats(st[:, b, :], src[:, b, :])
                last.then_inc(M[s_st], 1)
                dve.wait_ge(M[s_st], g + 1)
                dve.nop(nofuse=True)
                for b in range(G):
                    last = nc.vector.bn_aggr(mom[:, b, :], st[:, b, :])
                last.then_inc(M[s_mv], 1)
                dve.wait_ge(M[s_mv], g + 1)
                nc.vector.tensor_scalar(var[:], mom[:, :, 1], LN_EPS, None, ALU.add).then_inc(M[s_var], 1)

            def light_work(i, k, u):
                g = i - TAIL
                for (name, stage), at in zip(PROJ_USES, PROJ_AT):
                    if at == (k, u) and on(i, stage) and name in ("sqk", "cqk"):
                        split_lo(i, name, name[0])
                    if at == (k, u - 1) and on(i, stage) and name[1] in "qk" and name[2:] in ("0", "1"):
                        widen(i, name)
                if (k, u) == (0, 0) and on(i, CROSS):
                    store_v(i, "cv", "c", R_CVB)
                if (k, u) == (1, 0) and on(i, TAIL):
                    dve.wait_ge(M["cn_loaded"], 16 * (g + 1))
                    nc.vector.tensor_scalar(e_k[:], cn_in[:, :, 0:D], 0.0, None, ALU.min).then_inc(M["mink_ready"], 1)
                if (k, u) == (1, 2) and on(i, TAIL):
                    dve.wait_ge(M["expk_ready"], g + 1)
                    nc.vector.scalar_tensor_tensor(phi_k[:], e_k[:], 1.0, cn_in[:, :, 0:D], ALU.subtract,
                                                   ALU.max).then_inc(M["phik_ready"], 1)
                if (k, u) == (1, 4) and on(i, TAIL):
                    wait_full(dve, i, "ff")
                    dve.wait_ge(M["res_ready"], job_index(i, 0))
                    nc.vector.tensor_tensor(x3[:], proj_ps[:, 0:G * D].rearrange("p (b d) -> p b d", b=G),
                                            r2[:, bass.ds(g * G, G), :], ALU.add).then_inc(M["proj_read"], 1)
                    wait_read(dve, i, "ff")
                    norm_stats(x3, st6_f, mv_f, var_f, ("st3_ready", "mv3_ready", "var3_ready"), g)
                if (k, u) == (2, 3) and on(i, NEXT):
                    store_v(i, "sv", "s", R_SVB)
                if (k, u) == (2, 1) and on(i, TAIL):
                    dve.wait_ge(M["rstd3_ready"], g + 1)
                    wait_reuse(dve, M["y3g_ready"], g)
                    for b in range(G):
                        last = nc.vector.tensor_scalar(y3[:, b, :], x3[:, b, :], mv_f[:, b, 0:1], rstd_f[:, b:b + 1],
                                                       ALU.subtract, ALU.mult)
                    last.then_inc(M["y3_ready"], 1)
                if (k, u) == (3, 0) and on(i, TAIL):
                    wait_read(dve, i, "yt")
                    nc.vector.tensor_scalar(e_q[:], x3_t[:], 0.0, None, ALU.min).then_inc(M["minq_ready"], 1)
                if (k, u) == (3, 1) and on(i, TAIL):
                    dve.wait_ge(M["expq_ready"], g + 1)
                    nc.vector.scalar_tensor_tensor(phi_q[:], e_q[:], 1.0, x3_t[:], ALU.subtract, ALU.max).then_inc(
                        M["phiq_ready"], 1)
                if (k, u) == (3, 4) and on(i, TAIL):
                    wait_full(dve, i, "la")
                    la = proj_ps[:, 0:G * (D + 1)].rearrange("p (b n) -> p b n", b=G)
                    nc.vector.tensor_scalar(den[:], la[:, :, D], DEN_EPS, None, ALU.add).then_inc(M["den_ready"], 1)
                    dve.wait_ge(M["den_ready"], g + 1)
                    nc.vector.reciprocal(rec4[:], den[:]).then_inc(M["rec4_ready"], 1)
                    dve.wait_ge(M["rec4_ready"], g + 1)
                    dve.wait_ge(M["r3_ready"], g + 1)
                    for b in range(G):
                        last = nc.vector.scalar_tensor_tensor(x4[:, b, :].unsqueeze(1), la[:, b:b + 1, 0:D],
                                                              rec4[:, b:b + 1], r3[:, bass.ds(g * G + b, 1), :],
                                                              ALU.mult, ALU.add)
                    last.then_inc(M["proj_read"], 1)
                    wait_read(dve, i, "la")
                    norm_stats(x4, st6_l, mv_l, var_l, ("st4_ready", "mv4_ready", "var4_ready"), g)
                    dve.wait_ge(M["rstd4_ready"], g + 1)
                    wait_reuse(dve, M["y4g_ready"], g)
                    for b in range(G):
                        last = nc.vector.tensor_scalar(y4[:, b, :], x4[:, b, :], mv_l[:, b, 0:1], rstd_l[:, b:b + 1],
                                                       ALU.subtract, ALU.mult)
                    last.then_inc(M["y4_ready"], 1)

            def iteration(i):
                if static(i) and i == SELF:
                    dve.wait_ge(M["r0_ready"], 1)
                for k in range(4):
                    cur, nxt, prev, prev_y = schedule(i, k)
                    for u in range(UNITS):
                        if nxt:
                            max_unit(*nxt, u)
                            if u == UNITS - 1:
                                split_max(*nxt)
                        if u == 1 and prev:
                            normalise(*prev)
                        if u == 3 and prev:
                            residual(*prev)
                        light_work(i, k, u)
                    if prev:
                        standardise(*prev)
                    if nxt:
                        widen_max(*nxt)
                    light_work(i, k, UNITS)

            run_iterations(dve, iteration)

        @block.gpsimd
        def _(pool):
            nc.gpsimd.memset(neg_half[:], -0.5).then_inc(M["half_set"], 1)
            pool.wait_ge(M["half_set"], 1)
            pool.wait_ge(M["rows_in"], 16)
            pool.wait_ge(M["xall_in"], 16)

            def row(r, n):
                return row_sb[:, r:r + 1, :].to_broadcast([P, n, P])

            nc.gpsimd.tensor_tensor(r0[:], x_all[:], row(R_SOB, B), ALU.add).then_inc(M["r0_ready"], 1)
            nc.gpsimd.tensor_tensor(res_bias[:, 0, :], row_sb[:, R_E1, :], row_sb[:, R_COB, :], ALU.add)
            nc.gpsimd.tensor_tensor(res_bias[:, 1, :], row_sb[:, R_E2, :], row_sb[:, R_B2, :], ALU.add).then_inc(
                M["resb_set"], 1)
            pool.wait_ge(M["resb_set"], 1)

            def inverse_root(kind, b, g, job):
                pool.wait_ge(M["var_ready"], job + 1)
                nc.gpsimd.tensor_tensor(rstd[:, b, :], var_e[:, b, :], neg_half[:, 0:1], ALU.pow).then_inc(
                    M["rstd_ready"], 1)

            def next_residual(kind, b, g, job):
                gain, n, res = (R_G1, 0, r1) if kind == "s" else (R_G2, 1, r2)
                pool.wait_ge(M["yn_ready"], job + 1)
                nc.gpsimd.tensor_tensor(y_g[:], y_n[:, b, :], row_sb[:, gain, :], ALU.mult).then_inc(M["yg_ready"], 1)
                pool.wait_ge(M["yg_ready"], job + 1)
                nc.gpsimd.tensor_tensor(res[:, bass.ds(g * G + b, 1), :], y_g[:].unsqueeze(1),
                                        res_bias[:, n:n + 1, :], ALU.add).then_inc(M["res_ready"], 1)

            def iteration(i):
                g = i - TAIL
                for k in range(4):
                    cur, nxt, prev, prev_y = schedule(i, k)
                    if k == 2 and on(i, TAIL):
                        pool.wait_ge(M["var3_ready"], g + 1)
                        nc.gpsimd.tensor_tensor(rstd_f[:], var_f[:], neg_half[:], ALU.pow).then_inc(
                            M["rstd3_ready"], 1)
                    if prev:
                        inverse_root(*prev)
                        next_residual(*prev)
                    if k == 2 and on(i, TAIL):
                        pool.wait_ge(M["y3_ready"], g + 1)
                        nc.gpsimd.tensor_tensor(y3_g[:], y3[:], row(R_G3, G), ALU.mult).then_inc(M["y3g_ready"], 1)
                        pool.wait_ge(M["y3g_ready"], g + 1)
                        nc.gpsimd.tensor_tensor(r3[:, bass.ds(g * G, G), :], y3_g[:], row(R_E3, G), ALU.add).then_inc(
                            M["r3_ready"], 1)
                    if k == 3 and on(i, TAIL):
                        pool.wait_ge(M["var4_ready"], g + 1)
                        nc.gpsimd.tensor_tensor(rstd_l[:], var_l[:], neg_half[:], ALU.pow).then_inc(
                            M["rstd4_ready"], 1)
                        pool.wait_ge(M["y4_ready"], g + 1)
                        nc.gpsimd.tensor_tensor(y4_g[:], y4[:], row(R_GAM, G), ALU.mult).then_inc(M["y4g_ready"], 1)
                        pool.wait_ge(M["y4g_ready"], g + 1)
                        nc.gpsimd.tensor_tensor(o_all[:, bass.ds(g * G, G), :], y4_g[:], row(R_BET, G),
                                                ALU.add).then_inc(M["out_ready"], 1)

            run_iterations(pool, iteration)


def kernel(**inputs):
    import numpy as np
    import concourse.bacc as bacc
    from concourse.bass_utils import run_bass_kernel_spmd

    a = {k.replace("L0_xattn_", "").replace("L1_xattn_", ""): np.asarray(v) for k, v in inputs.items()}
    x, c, mask = a["x"], a["ctx_1024"], a["mask_1x1xSxS_ik0"][0, 0]
    b, s, d = x.shape
    sk = c.shape[1]
    square = ["sa_qw", "sa_kw", "sa_vw", "sa_ow", "ca_qw", "ca_kw", "ca_vw", "ca_ow"]
    nf = a["w1"].shape[1] // P
    blocks = [a[n] for n in square] + [a["w1"][:, P * n:P * n + P] for n in range(nf)] + \
             [a["w2"][P * n:P * n + P] for n in range(nf)]
    columns = [a["sa_qb"], a["sa_kb"], a["ca_qb"], a["ca_kb"]] + [a["b1"][P * n:P * n + P] for n in range(nf)] + \
              [a[n] for n in ("g1", "be1", "g2", "be2", "g3", "be3")]
    rows = [a[n] for n in ("sa_vb", "sa_ob", "ca_vb", "ca_ob", "b2", "g1", "be1", "g2", "be2", "g3", "be3", "gamma",
                           "beta")]
    data = {
        "x": x,
        "x_t": x.reshape(b // G, G, s, d).transpose(0, 3, 1, 2),
        "ctx_n": c,
        "ctx_t": c.reshape(b // G, G, sk, d).transpose(0, 3, 1, 2),
        "mask_q": mask,
        "mask_k": mask.T,
        "weights": np.stack(blocks, axis=1),
        "cols": np.stack(columns, axis=1),
        "rows": np.stack(rows),
        "ident": np.eye(P, dtype=np.float32),
    }
    data = {n: np.ascontiguousarray(v) for n, v in data.items()}
    nc = bacc.Bacc("TRN2", target_bir_lowering=False, num_devices=1)
    args = [nc.dram_tensor("in_" + n, v.shape, mybir.dt.from_np(v.dtype), kind="ExternalInput").ap()
            for n, v in data.items()]
    out = nc.dram_tensor("out", (b, s, d), F32, kind="ExternalOutput").ap()
    decoder_layer_kernel(nc, *args, out)
    r = run_bass_kernel_spmd(nc, [{"in_" + n: v for n, v in data.items()}], core_ids=[0])
    return r.results[0]["out"]
```

```python
from contextlib import ExitStack

import concourse.bass as bass
from concourse import mybir

F32 = mybir.dt.float32
BF16 = mybir.dt.bfloat16
I32 = mybir.dt.int32
ALU = mybir.AluOpType
ACT = mybir.ActivationFunctionType
AX_X = mybir.AxisListType.X
AX_XY = mybir.AxisListType.XY

P = 128
NH = 16
HD = 8
UNITS = 4
RH = 4
G = 2
MASKED = -float(2 ** 48)
LN_EPS = 1e-5
DEN_EPS = 1e-6
VW = 32

C_SQB, C_SKB, C_CQB, C_CKB, C_B1, C_G1, C_E1, C_G2, C_E2, C_G3, C_E3 = 0, 1, 2, 3, 4, 8, 9, 10, 11, 12, 13
N_COLS = 14
R_SVB, R_SOB, R_CVB, R_COB, R_B2, R_G1, R_E1, R_G2, R_E2, R_G3, R_E3, R_GAM, R_BET = range(13)
N_ROWS = 13
W_SQ, W_SK, W_SV, W_SO, W_CQ, W_CK, W_CV, W_CO, W_1, W_2 = 0, 1, 2, 3, 4, 5, 6, 7, 8, 12
N_W = 16


def decoder_layer_kernel(nc, x, x_t, ctx_n, ctx_t, mask_q, mask_k, weights, cols, rows, ident, out):
    B, S, D = x.shape
    SK = ctx_n.shape[1]
    NG = B // G
    NF = 4
    SCALE = 1.0 / float(HD) ** 0.5
    KLEN = {"s": S, "c": SK}

    NEXT, SELF, CROSS, TAIL, LAST = -1, 0, 1, 2, 3

    def static(i):
        return isinstance(i, int)

    def on(i, first):
        return 0 <= i - first < NG if static(i) else True

    def begun(i, first):
        return min(max(i - first, 0), NG) if static(i) else i - first

    def count(i, firsts, at):
        if static(i):
            return sum(begun(i, f) for f in firsts) + sum(int(on(i, f)) for f in firsts[:at])
        return i * len(firsts) + (at - sum(firsts))

    JOB_STAGES = [SELF, SELF, CROSS, CROSS]

    def job_index(i, k):
        return count(i, JOB_STAGES, k)

    def schedule(i, k):
        def job(at, back=0):
            if at >= 4:
                return job(at - 4, back - 1)
            if at < 0:
                return job(at + 4, back + 1)
            first = JOB_STAGES[at]
            if not on(i - back, first):
                return None
            return ("s" if first == SELF else "c", at % 2, i - back - first, job_index(i - back, at))
        return job(k), job(k + 1), job(k - 1), job(k - 2)

    PROJ_USES = [
        ("yc0", TAIL, 0, 0), ("cv", CROSS, 0, 0), ("cq0", CROSS, 0, 1), ("ck0", CROSS, 0, 2), ("sqk", NEXT, 0, 3),
        ("yc1", TAIL, 1, 0), ("cq1", CROSS, 1, 0), ("ck1", CROSS, 1, 1), ("h01", TAIL, 1, 1), ("h23", TAIL, 1, 2),
        ("ff", TAIL, 1, 4),
        ("ys0", SELF, 2, 0), ("sq0", NEXT, 2, 0), ("sk0", NEXT, 2, 1), ("kv", TAIL, 2, 2), ("sv", NEXT, 2, 3),
        ("yt", TAIL, 2, 4),
        ("ys1", SELF, 3, 0), ("sq1", NEXT, 3, 0), ("sk1", NEXT, 3, 1), ("cqk", SELF, 3, 2), ("la", TAIL, 3, 3)]
    USE_NAMES = [name for name, *_ in PROJ_USES]

    def bank_of(name):
        return USE_NAMES.index(name) % 2

    def use_index(i, name):
        bank = bank_of(name)
        return count(i, [stage for _, stage, *_ in PROJ_USES[bank::2]], USE_NAMES[bank::2].index(name))

    def uses_at(i, k, u):
        return [name for name, stage, *at in PROJ_USES if tuple(at) == (k, u) and on(i, stage)]

    def is_spread(name):
        return name[1] in "qk" and name[2] in "01"

    def maxima_at(u):
        return [0, 1] if u == 0 else [u + 1] if u < UNITS - 1 else []

    def wait_reuse(eng, sem, value):
        if not static(value) or value > 0:
            eng.wait_ge(sem, value)

    def run_iterations(eng, iteration):
        for i in range(NEXT, TAIL + 1):
            iteration(i)
        with eng.Fori(TAIL + 1, NG - 1) as i:
            iteration(i)
        for i in range(NG - 1, NG + LAST):
            iteration(i)

    with ExitStack() as ctx:
        def sb(name, shape, dt=F32):
            return ctx.enter_context(nc.sbuf_tensor(name, shape, dt))

        def psum(name, shape, dt=F32):
            return ctx.enter_context(nc.psum_tensor(name, shape, dt))

        def sem(name):
            return ctx.enter_context(nc.semaphore(name))

        w_sb = sb("w_sb", [P, N_W, P])
        col_sb = sb("col_sb", [P, N_COLS])
        row_sb = sb("row_sb", [P, N_ROWS, P])
        id_f = sb("id_f", [P, P])
        id_b = sb("id_b", [P, P], BF16)
        spread = {(side, part): sb(f"spread_{side}_{part}", [P, UNITS, 4, 32], BF16)
                  for side in "qk" for part in ("hi", "lo")}
        row_is_j = sb("row_is_j", [P, RH])
        max_is_j = sb("max_is_j", [P, RH])
        max_is_u = sb("max_is_u", [P, UNITS])
        unit_sel = sb("unit_sel", [P, UNITS, P], BF16)
        mask_q_i = sb("mask_q_i", [P, S], I32)
        mask_k_i = sb("mask_k_i", [P, S], I32)
        bias_q = sb("bias_q", [P, S], BF16)
        bias_k = sb("bias_k", [P, S], BF16)
        neg_half = sb("neg_half", [P, G])
        warm = sb("warm", [P, G])
        res_bias = sb("res_bias", [P, 2, P])
        x_all = sb("x_all", [P, B, D])
        r0 = sb("r0", [P, B, D])
        r1 = sb("r1", [P, B, D])
        r2 = sb("r2", [P, B, D])
        r3 = sb("r3", [P, B, D])
        o_all = sb("o_all", [P, B, D])
        xt_in = sb("xt_in", [P, G, S])
        ct_in = sb("ct_in", [P, G, SK])
        cn_in = sb("cn_in", [SK, G, D + 1])
        hi, lo, rows_qk, wide = {}, {}, {}, {}
        for kind in "sc":
            for side in "qk":
                n = KLEN[kind] if side == "k" else S
                key = kind + side
                hi[key] = sb(f"{key}_hi", [P, G, n], BF16)
                lo[key] = sb(f"{key}_lo", [P, G, n], BF16)
                rows_qk[key] = sb(f"{key}_rows", [P, G, UNITS, n], BF16)
            wide[kind] = sb(f"{kind}q_wide", [P, G, RH, UNITS, S], BF16)
        v_aug = {"s": sb("v_aug_s", [S, G, UNITS, RH, VW]), "c": sb("v_aug_c", [SK, G, UNITS, RH, VW])}
        neg_max = sb("neg_max", [P, 2, NH])
        nm_parts = sb("nm_parts", [P, P], BF16)
        max_x = sb("max_x", [P, 2, RH, S], BF16)
        probs = sb("probs", [P, 2, RH * S])
        av_sb = sb("av_sb", [P, 2, 2 * S])
        rden = sb("rden", [P, 2, NH])
        att = sb("att", [P, 2, D])
        att_t = sb("att_t", [P, 2, S])
        x_post = sb("x_post", [P, 2, D])
        st6 = sb("st6", [P, 2, 6])
        mv = sb("mv", [P, 2, 2])
        var_e = sb("var_e", [P, 2, 1])
        rstd = sb("rstd", [P, 2, 1])
        y_n = sb("y_n", [P, 2, D])
        y_g = sb("y_g", [P, D])
        x1_t = sb("x1_t", [P, G, S])
        x2_t = sb("x2_t", [P, G, S])
        hid = sb("hid", [P, NF, G, S])
        x3 = sb("x3", [P, G, D])
        st6_f = sb("st6_f", [P, G, 6])
        mv_f = sb("mv_f", [P, G, 2])
        var_f = sb("var_f", [P, G])
        rstd_f = sb("rstd_f", [P, G])
        y3 = sb("y3", [P, G, D])
        y3_g = sb("y3_g", [P, G, D])
        x3_t = sb("x3_t", [P, G, S])
        e_q = sb("e_q", [P, G, S])
        phi_q = sb("phi_q", [P, G, S])
        e_k = sb("e_k", [SK, G, D])
        phi_k = sb("phi_k", [SK, G, D])
        kv_sb = sb("kv_sb", [P, G, D + 1])
        den = sb("den", [P, G])
        rec4 = sb("rec4", [P, G])
        x4 = sb("x4", [P, G, D])
        st6_l = sb("st6_l", [P, G, 6])
        mv_l = sb("mv_l", [P, G, 2])
        var_l = sb("var_l", [P, G])
        rstd_l = sb("rstd_l", [P, G])
        y4 = sb("y4", [P, G, D])

        s1_ps = [psum(f"s1_ps{n}", [P, RH * S]) for n in range(2)]
        s2_ps = [psum(f"s2_ps{n}", [P, RH * S]) for n in range(2)]
        av_ps = psum("av_ps", [P, 2 * S])
        post_ps = psum("post_ps", [P, 4, S])
        proj_ps = [psum(f"proj_ps{n}", [P, RH * S]) for n in range(2)]

        names = """w_first w_second w_rest cols_in rows_in ident_in mask_in xall_in xt_loaded ct_loaded cn_loaded
            stored
            id_set bias_set spread_set masks_set unit_set zeros_set half_set r0_ready resb_set
            s1_ready max_done nm_hi nm_ready nmt_ready maxt_ready s2_ready exp_done av_ready av_copied
            pvt_ready rden_ready att_ready attt_ps attt_ready o_ready xpost_ready st_ready mv_ready var_ready
            rstd_ready yn_ready yg_ready res_ready
            proj_full0 proj_read0 proj_full1 proj_read1
            hi_sqk hi_cqk wide_s wide_c
            st3_ready mv3_ready var3_ready rstd3_ready y3_ready y3g_ready r3_ready
            minq_ready expq_ready phiq_ready mink_ready expk_ready phik_ready
            den_ready rec4_ready st4_ready mv4_ready var4_ready rstd4_ready y4_ready out_ready"""
        M = {n: sem(n) for n in names.split()}

        nmt_ps = s1_ps[1][:, 0:P // 2].bitcast(BF16)

        def wait_full(eng, i, name):
            eng.wait_ge(M[f"proj_full{bank_of(name)}"], use_index(i, name) + 1)

        def wait_read(eng, i, name):
            eng.wait_ge(M[f"proj_read{bank_of(name)}"], use_index(i, name) + 1)

        def full(name):
            return M[f"proj_full{bank_of(name)}"]

        def read(name):
            return M[f"proj_read{bank_of(name)}"]

        def wait_rows(eng, kind, side, b, g):
            wait_read(eng, g + (NEXT if kind == "s" else CROSS), kind + side + str(b))

        block = ctx.enter_context(nc.Block())

        @block.sync
        def _(sp):
            def load_xt(g):
                sp.dma_start(xt_in[:], x_t[bass.ds(g, 1)].rearrange("a p b n -> (a p) b n")).then_inc(
                    M["xt_loaded"], 16)

            def settle():
                sp.nop(nofuse=True)

            load_xt(0)
            sp.dma_start(w_sb[:, 0:2, :], weights[:, 0:2, :]).then_inc(M["w_first"], 16)
            sp.dma_start(mask_q_i[:], mask_q).then_inc(M["mask_in"], 16)
            sp.dma_start(w_sb[:, 2:4, :], weights[:, 2:4, :]).then_inc(M["w_second"], 16)
            sp.dma_start(row_sb[:], rows.unsqueeze(0).to_broadcast([P, N_ROWS, P])).then_inc(M["rows_in"], 16)
            sp.dma_start(x_all[:], x.rearrange("b p d -> p b d")).then_inc(M["xall_in"], 16)
            sp.dma_start(w_sb[:, 4:N_W, :], weights[:, 4:N_W, :]).then_inc(M["w_rest"], 16)

            def iteration(i):
                if on(i, NEXT) and (not static(i) or i > NEXT):
                    wait_full(sp, i - 1, "sv")
                    settle()
                    load_xt(i - NEXT)
                if on(i, TAIL):
                    wait_reuse(sp, M["phik_ready"], i - TAIL)
                    settle()
                    if not static(i) or i > TAIL:
                        wait_read(sp, i - 1, "kv")
                    settle()
                    sp.dma_start(cn_in[:, :, 0:D], ctx_n[bass.ds((i - TAIL) * G, G)].rearrange(
                        "b k d -> k b d")).then_inc(M["cn_loaded"], 16)
                if on(i, SELF):
                    if on(i, CROSS):
                        wait_full(sp, i, "cv")
                    settle()
                    sp.dma_start(ct_in[:], ctx_t[bass.ds(i, 1)].rearrange("a p b n -> (a p) b n")).then_inc(
                        M["ct_loaded"], 16)
                if on(i, LAST):
                    g = i - LAST
                    sp.wait_ge(M["out_ready"], g + 1)
                    settle()
                    sp.dma_start(out[bass.ds(g * G, G)].rearrange("b p d -> p b d"),
                                 o_all[:, bass.ds(g * G, G), :]).then_inc(M["stored"], 16)

            run_iterations(sp, iteration)
            sp.wait_ge(M["stored"], 16 * NG)

        @block.tensor
        def _(pe):
            pe.wait_ge(M["w_first"], 16)

            def query_major(kind, b, g, job, u):
                n = KLEN[kind]
                if u == 0:
                    pe.wait_ge(M[f"wide_{kind}"], G * g + b + 1)
                    wait_rows(pe, kind, "k", b, g)
                wait_reuse(pe, M["max_done"], job * UNITS + u - 1)
                if u == 1:
                    wait_reuse(pe, M["maxt_ready"], job)
                bank = s1_ps[u % 2]
                if kind == "s":
                    nc.tensor.matmul(bank[:, :], id_b[:], bias_q[:].unsqueeze(1).to_broadcast([P, RH, n]),
                                     start=True, stop=False, skip_group_check=True)
                for j in range(RH):
                    last = nc.tensor.matmul(bank[:, j * n:(j + 1) * n], wide[kind][:, b, j, u, :],
                                            rows_qk[kind + "k"][:, b, u, :], start=(kind == "c"), stop=True,
                                            skip_group_check=True)
                last.then_inc(M["s1_ready"], 1)

            def transpose_max(job):
                pe.wait_ge(M["nm_ready"], job + 1)
                nc.tensor.transpose(nmt_ps, nm_parts[:], id_b[:]).then_inc(M["nmt_ready"], 1)

            def key_major(kind, b, g, job, u):
                n = KLEN[kind]
                wait_reuse(pe, M["exp_done"], job * UNITS + u - 1)
                bank = s2_ps[u % 2]
                if kind == "s":
                    nc.tensor.matmul(bank[:, :], id_b[:], bias_k[:].unsqueeze(1).to_broadcast([P, RH, S]),
                                     start=True, stop=False)
                nc.tensor.matmul(bank[0:n, :], rows_qk[kind + "k"][:, b, u, :], wide[kind][:, b, :, u, :],
                                 start=(kind == "c"), stop=False)
                if u == 0:
                    pe.wait_ge(M["maxt_ready"], job + 1)
                nc.tensor.matmul(bank[0:n, :], unit_sel[:, u, 0:n], max_x[:, b, :, :], start=False,
                                 stop=True).then_inc(M["s2_ready"], 1)

            def times_v(i, kind, b, g, job, u):
                if u == 0:
                    wait_reuse(pe, M["av_copied"], job)
                    if b == 0:
                        wait_read(pe, i if kind == "c" else i - 1, kind + "v")
                pe.wait_ge(M["exp_done"], job * UNITS + u + 1)
                a, rr = u // 2, u % 2
                for r in range(RH):
                    last = nc.tensor.matmul(av_ps[32 * r:32 * r + VW, rr * S:(rr + 1) * S],
                                            v_aug[kind][:, b, u, r, :], probs[0:KLEN[kind], u % 2, r * S:(r + 1) * S],
                                            start=(u == 0), stop=(a == 1), skip_group_check=True)
                last.then_inc(M["av_ready"], 1)

            def post_transpose_pv(kind, b, g, job):
                pe.wait_ge(M["av_copied"], job + 1)
                wait_reuse(pe, M["xpost_ready"], job)
                for rr in range(2):
                    last = nc.tensor.transpose(post_ps[:, rr, :], av_sb[:, b, rr * S:(rr + 1) * S], id_f[:])
                last.then_inc(M["pvt_ready"], 1)

            def post_transpose_att(kind, b, g, job):
                pe.wait_ge(M["att_ready"], job + 1)
                nc.tensor.transpose(post_ps[:, 2, :], att[:, b, :], id_f[:]).then_inc(M["attt_ps"], 1)

            def post_project(kind, b, g, job):
                pe.wait_ge(M["attt_ready"], job + 1)
                nc.tensor.matmul(post_ps[:, 3, :], att_t[:, b, :], w_sb[:, W_SO if kind == "s" else W_CO, :],
                                 start=True, stop=True).then_inc(M["o_ready"], 1)

            def open_bank(i, name):
                wait_reuse(pe, read(name), use_index(i, name))
                return proj_ps[bank_of(name)]

            def project_t(bank, w, src, at, n):
                return nc.tensor.matmul(bank[:, at:at + n], w_sb[:, w, :], src, start=True, stop=True)

            def project_v(i, name, w, src, n):
                bank = open_bank(i, name)
                for b in range(G):
                    last = nc.tensor.matmul(bank[0:n, b * D:(b + 1) * D], src[:, b, :], w_sb[:, w, :],
                                            start=True, stop=True)
                last.then_inc(full(name), 1)

            def project_qk(i, name, w_q, q_src, w_k, k_src, n):
                bank = open_bank(i, name)
                project_t(bank, w_q, q_src, 0, G * S)
                project_t(bank, w_k, k_src, G * S, G * n).then_inc(full(name), 1)

            def mlp_up(i, name, c):
                bank = open_bank(i, name)
                project_t(bank, W_1 + c, x2_t[:], 0, G * S)
                project_t(bank, W_1 + c + 1, x2_t[:], G * S, G * S).then_inc(full(name), 1)

            def mlp_down(i):
                bank = open_bank(i, "ff")
                wait_read(pe, i, "h23")
                for b in range(G):
                    for c in range(NF):
                        last = nc.tensor.matmul(bank[:, b * D:(b + 1) * D], hid[:, c, b, :],
                                                w_sb[:, W_2 + c, :], start=(c == 0), stop=(c == NF - 1))
                last.then_inc(full("ff"), 1)

            def context_kv(i):
                pe.wait_ge(M["phik_ready"], i - TAIL + 1)
                bank = open_bank(i, "kv")
                for b in range(G):
                    last = nc.tensor.matmul(bank[:, b * (D + 1):(b + 1) * (D + 1)], phi_k[:, b, :], cn_in[:, b, :],
                                            start=True, stop=True)
                last.then_inc(full("kv"), 1)

            def transpose_y(i, name, job):
                pe.wait_ge(M["yn_ready"], job + 1)
                bank = open_bank(i, name)
                nc.tensor.transpose(bank[:, 0:S], y_n[:, int(name[2]), :], id_f[:]).then_inc(full(name), 1)

            def transpose_y3(i):
                pe.wait_ge(M["y3_ready"], i - TAIL + 1)
                bank = open_bank(i, "yt")
                for b in range(G):
                    last = nc.tensor.transpose(bank[:, b * S:(b + 1) * S], y3[:, b, :], id_f[:])
                last.then_inc(full("yt"), 1)

            def linear_attention(i):
                pe.wait_ge(M["phiq_ready"], i - TAIL + 1)
                bank = open_bank(i, "la")
                for b in range(G):
                    last = nc.tensor.matmul(bank[:, b * (D + 1):(b + 1) * (D + 1)], phi_q[:, b, :], kv_sb[:, b, :],
                                            start=True, stop=True)
                last.then_inc(full("la"), 1)

            def spread_rows(i, name):
                kind, side, b = name[0], name[1], int(name[2])
                n = KLEN[kind] if side == "k" else S
                wait_read(pe, i if kind == "s" else i - 1, kind + "qk")
                bank = open_bank(i, name)
                for u in range(UNITS):
                    nc.tensor.matmul(bank[:, u * n:(u + 1) * n], spread[side, "hi"][:, u, :, :],
                                     hi[kind + side][:, b, :], start=True, stop=False)
                    last = nc.tensor.matmul(bank[:, u * n:(u + 1) * n], spread[side, "lo"][:, u, :, :],
                                            lo[kind + side][:, b, :], start=False, stop=True)
                last.then_inc(full(name), 1)

            def light_work(i, k, u):
                prev_y = schedule(i, k)[3]
                for name in uses_at(i, k, u):
                    if name[0] == "y" and name != "yt":
                        transpose_y(i, name, prev_y[3])
                    elif name == "cv":
                        project_v(i, "cv", W_CV, ct_in, SK)
                    elif name == "sv":
                        if static(i) and i == NEXT:
                            pe.wait_ge(M["w_second"], 16)
                        project_v(i, "sv", W_SV, xt_in, S)
                    elif name == "sqk":
                        pe.wait_ge(M["xt_loaded"], 16 * (i - NEXT + 1))
                        project_qk(i, "sqk", W_SQ, xt_in[:], W_SK, xt_in[:], S)
                    elif name == "cqk":
                        pe.wait_ge(M["ct_loaded"], 16 * (i + 1))
                        wait_read(pe, i, "ys0")
                        wait_read(pe, i, "ys1")
                        project_qk(i, "cqk", W_CQ, x1_t[:], W_CK, ct_in[:], SK)
                    elif name == "h01":
                        wait_read(pe, i, "yc0")
                        wait_read(pe, i, "yc1")
                        mlp_up(i, "h01", 0)
                    elif name == "h23":
                        mlp_up(i, "h23", 2)
                    elif name == "ff":
                        mlp_down(i)
                    elif name == "kv":
                        context_kv(i)
                    elif name == "yt":
                        transpose_y3(i)
                    elif name == "la":
                        linear_attention(i)
                    elif is_spread(name):
                        if static(i) and i == NEXT:
                            pe.wait_ge(M["spread_set"], 1)
                        spread_rows(i, name)

            def iteration(i):
                if static(i) and i == SELF:
                    pe.wait_ge(M["w_rest"], 16)
                for k in range(4):
                    cur, nxt, prev, _ = schedule(i, k)
                    for u in range(UNITS):
                        ahead = maxima_at(u) if nxt else []
                        if static(i) and i == NEXT and k == 3 and u == 0:
                            pe.wait_ge(M["bias_set"], 1)
                            pe.wait_ge(M["unit_set"], 1)
                        for v in ahead[:1]:
                            query_major(*nxt, v)
                        if u == 0 and prev:
                            times_v(i, *prev, UNITS - 1)
                        if cur:
                            key_major(*cur, u)
                        for v in ahead[1:]:
                            query_major(*nxt, v)
                        if cur and u > 0:
                            times_v(i, *cur, u - 1)
                        if u == 3 and nxt:
                            transpose_max(nxt[3])
                        light_work(i, k, u)
                        if u == 0 and prev:
                            post_transpose_pv(*prev)
                        if u == 1 and prev:
                            post_transpose_att(*prev)
                        if u == 2 and prev:
                            post_project(*prev)
                    light_work(i, k, UNITS)

            run_iterations(pe, iteration)

        @block.scalar
        def _(act):
            act.dma_start(id_f[:], ident).then_inc(M["ident_in"], 16)
            act.dma_start(col_sb[:], cols).then_inc(M["cols_in"], 16)
            act.dma_start(mask_k_i[:], mask_k).then_inc(M["mask_in"], 16)
            act.wait_ge(M["half_set"], 1)
            nc.scalar.activation(warm[:], neg_half[:], ACT.Exp)
            act.wait_ge(M["cols_in"], 16)

            def col(c):
                return col_sb[:, c:c + 1]

            def exp_unit(kind, b, g, job, u):
                n = KLEN[kind]
                act.wait_ge(M["s2_ready"], job * UNITS + u + 1)
                wait_reuse(act, M["av_ready"], job * UNITS + u - 1)
                nc.scalar.activation(probs[0:n, u % 2, :], s2_ps[u % 2][0:n, :], ACT.Exp, scale=SCALE).then_inc(
                    M["exp_done"], 1)

            def copy_av(kind, b, g, job):
                act.wait_ge(M["av_ready"], (job + 1) * UNITS)
                wait_reuse(act, M["pvt_ready"], job - 1)
                nc.scalar.copy(av_sb[:, b, :], av_ps[:, :]).then_inc(M["av_copied"], 1)

            def copy_att(kind, b, g, job):
                act.wait_ge(M["attt_ps"], job + 1)
                wait_reuse(act, M["o_ready"], job - 1)
                nc.scalar.copy(att_t[:, b, :], post_ps[:, 2, :]).then_inc(M["attt_ready"], 1)

            def scale_y(i, name):
                kind, b = name[1], int(name[2])
                dst, gain, bias = (x1_t, C_G1, C_E1) if kind == "s" else (x2_t, C_G2, C_E2)
                wait_full(act, i, name)
                if name == "ys0" and (not static(i) or i > SELF):
                    wait_full(act, i - 1, "cqk")
                if name == "yc0" and (not static(i) or i > TAIL):
                    wait_full(act, i - 1, "h23")
                nc.scalar.activation(dst[:, b, :], proj_ps[bank_of(name)][:, 0:S], ACT.Identity, bias=col(bias),
                                     scale=col(gain)).then_inc(read(name), 1)

            def split_hi(i, name, kind):
                wait_full(act, i, name)
                for side, at, c in (("q", 0, C_SQB if kind == "s" else C_CQB),
                                    ("k", G * S, C_SKB if kind == "s" else C_CKB)):
                    dst = hi[kind + side]
                    n = dst.shape[2]
                    src = proj_ps[bank_of(name)][:, at:at + G * n].rearrange("p (b n) -> p b n", b=G)
                    last = nc.scalar.activation(dst[:], src, ACT.Identity, bias=col(c))
                last.then_inc(M["hi_" + name], 1)

            def copy_rows(i, name):
                kind, side, b = name[0], name[1], int(name[2])
                n = KLEN[kind] if side == "k" else S
                wait_full(act, i, name)
                wait_reuse(act, M["s2_ready"], UNITS * job_index(i, b + 1 if kind == "s" else 0))
                if side == "q":
                    g = i - (NEXT if kind == "s" else CROSS)
                    if not static(g) or g > 0:
                        act.wait_ge(M[f"wide_{kind}"], G * (g - 1) + b + 1)
                nc.scalar.copy(rows_qk[name[:2]][:, b, :, :], proj_ps[bank_of(name)][:, 0:UNITS * n].rearrange(
                    "p (u n) -> p u n", u=UNITS)).then_inc(read(name), 1)

            def relu(i, name, c):
                wait_full(act, i, name)
                if c == 0 and (not static(i) or i > TAIL):
                    wait_full(act, i - 1, "ff")
                for h in range(2):
                    last = nc.scalar.activation(
                        hid[:, c + h, :, :],
                        proj_ps[bank_of(name)][:, h * G * S:(h + 1) * G * S].rearrange("p (b n) -> p b n", b=G),
                        ACT.Relu, bias=col(C_B1 + c + h))
                last.then_inc(read(name), 1)

            def light_work(i, k, u):
                if (k, u) == (1, 0) and on(i, TAIL):
                    act.wait_ge(M["mink_ready"], i - TAIL + 1)
                    nc.scalar.activation(e_k[:], e_k[:], ACT.Exp).then_inc(M["expk_ready"], 1)
                if (k, u) == (3, 0) and on(i, TAIL):
                    act.wait_ge(M["minq_ready"], i - TAIL + 1)
                    nc.scalar.activation(e_q[:], e_q[:], ACT.Exp).then_inc(M["expq_ready"], 1)
                for name in uses_at(i, k, u):
                    bank = proj_ps[bank_of(name)]
                    if name[0] == "y" and name != "yt":
                        scale_y(i, name)
                    elif name in ("sqk", "cqk"):
                        split_hi(i, name, name[0])
                    elif name == "h01":
                        relu(i, name, 0)
                    elif name == "h23":
                        relu(i, name, 2)
                    elif name == "kv":
                        wait_full(act, i, "kv")
                        if not static(i) or i > TAIL:
                            wait_full(act, i - 1, "la")
                        nc.scalar.copy(kv_sb[:], bank[:, 0:G * (D + 1)].rearrange("p (b n) -> p b n", b=G)).then_inc(
                            read("kv"), 1)
                    elif name == "yt":
                        wait_full(act, i, "yt")
                        wait_reuse(act, M["phiq_ready"], i - TAIL)
                        nc.scalar.activation(x3_t[:], bank[:, 0:G * S].rearrange("p (b n) -> p b n", b=G),
                                             ACT.Identity, bias=col(C_E3), scale=col(C_G3)).then_inc(read("yt"), 1)
                    elif is_spread(name):
                        copy_rows(i, name)

            def iteration(i):
                for k in range(4):
                    cur, _, prev, _ = schedule(i, k)
                    if prev:
                        copy_av(*prev)
                    for u in range(UNITS):
                        if cur:
                            exp_unit(*cur, u)
                        light_work(i, k, u)
                        if u == 1 and prev:
                            copy_att(*prev)
                    light_work(i, k, UNITS)

            run_iterations(act, iteration)

        @block.vector
        def _(dve):
            nc.vector.memset(nm_parts[:], 0.0)
            for kind in "sc":
                nc.vector.memset(v_aug[kind][:], 0.0)
            for tile in spread.values():
                nc.vector.memset(tile[:], 0.0)
            nc.vector.memset(cn_in[:, :, D:D + 1], 1.0).then_inc(M["zeros_set"], 1)
            dve.wait_ge(M["zeros_set"], 1)
            for kind in "sc":
                for a in range(2):
                    nc.vector.memset(v_aug[kind][:, :, 2 * a:2 * a + 2, :, 9 * a + HD:9 * a + HD + 1], 1.0)
            dve.wait_ge(M["ident_in"], 16)
            nc.vector.tensor_copy(id_b[:], id_f[:]).then_inc(M["id_set"], 1)
            dve.wait_ge(M["id_set"], 1)
            for (side, part), tile in spread.items():
                for s in range(4):
                    if (s // 2 if side == "q" else s % 2) == (part == "lo"):
                        last = nc.vector.tensor_copy(tile[:, :, s, :], id_b[:].rearrange("p (u m) -> p u m", u=UNITS))
            last.then_inc(M["spread_set"], 1)
            by_row = id_f[:].rearrange("p (s j i) -> p j s i", s=4, j=RH)
            by_head = id_f[:, 0:2 * NH].rearrange("p (c u j) -> p c u j", c=2, u=UNITS)
            nc.vector.tensor_reduce(row_is_j[:], by_row, AX_XY, ALU.add)
            nc.vector.tensor_reduce(max_is_j[:], by_head.rearrange("p c u j -> p j c u"), AX_XY, ALU.add)
            nc.vector.tensor_reduce(max_is_u[:], by_head.rearrange("p c u j -> p u c j"), AX_XY, ALU.add).then_inc(
                M["masks_set"], 1)
            dve.wait_ge(M["masks_set"], 1)
            nc.vector.tensor_copy(unit_sel[:], max_is_u[:].unsqueeze(2).to_broadcast([P, UNITS, P])).then_inc(
                M["unit_set"], 1)
            dve.wait_ge(M["mask_in"], 32)
            nc.vector.tensor_scalar(bias_k[:], mask_k_i[:], 0.0, MASKED, ALU.is_equal, ALU.mult)
            nc.vector.tensor_scalar(bias_q[:], mask_q_i[:], 0.0, MASKED, ALU.is_equal, ALU.mult).then_inc(
                M["bias_set"], 1)
            dve.wait_ge(M["cols_in"], 16)

            def col(c):
                return col_sb[:, c:c + 1]

            def max_unit(kind, b, g, job, u):
                n = KLEN[kind]
                dve.wait_ge(M["s1_ready"], job * UNITS + u + 1)
                scores = s1_ps[u % 2][:, 0:RH * n].rearrange("p (j n) -> p j n", j=RH)
                nc.vector.tensor_reduce(neg_max[:, b, RH * u:RH * (u + 1)], scores, AX_X, ALU.max, negate=True).then_inc(M["max_done"], 1)

            def split_max(kind, b, g, job):
                dve.wait_ge(M["max_done"], (job + 1) * UNITS)
                wait_reuse(dve, M["nmt_ready"], job)
                nc.vector.tensor_copy(nm_parts[:, 0:NH], neg_max[:, b, :]).then_inc(M["nm_hi"], 1)
                dve.wait_ge(M["nm_hi"], job + 1)
                nc.vector.tensor_tensor(nm_parts[:, NH:2 * NH], neg_max[:, b, :], nm_parts[:, 0:NH],
                                        ALU.subtract).then_inc(M["nm_ready"], 1)

            def widen_max(kind, b, g, job):
                dve.wait_ge(M["nmt_ready"], job + 1)
                wait_reuse(dve, M["s2_ready"], (job - 1) * UNITS)
                nc.vector.tensor_tensor(max_x[:, b, :, :], nmt_ps.unsqueeze(1).to_broadcast([P, RH, S]),
                                        max_is_j[:].unsqueeze(2).to_broadcast([P, RH, S]), ALU.mult).then_inc(
                    M["maxt_ready"], 1)

            def normalise(kind, b, g, job):
                pv = post_ps[:, 0:2, :].rearrange("q rr (r w) -> q (rr r) w", w=VW)[:, :, 0:2 * (HD + 1)].rearrange(
                    "q h (a w) -> q h a w", a=2)
                rd = rden[:, b, :].rearrange("q (h a) -> q h a", a=2)
                dve.wait_ge(M["pvt_ready"], job + 1)
                nc.vector.reciprocal(rd, pv[:, :, :, HD]).then_inc(M["rden_ready"], 1)
                dve.wait_ge(M["rden_ready"], job + 1)
                wait_reuse(dve, M["attt_ps"], job - 1)
                nc.vector.tensor_tensor(att[:, b, :].rearrange("q (a h d) -> q h a d", a=2, d=HD), pv[:, :, :, 0:HD],
                                        rd.unsqueeze(3).to_broadcast([P, 2 * RH, 2, HD]), ALU.mult).then_inc(
                    M["att_ready"], 1)

            def residual(kind, b, g, job):
                res = r0 if kind == "s" else r1
                dve.wait_ge(M["o_ready"], job + 1)
                if kind == "c":
                    dve.wait_ge(M["res_ready"], job - 3)
                nc.vector.tensor_tensor(x_post[:, b, :].unsqueeze(1), post_ps[:, 3, :].unsqueeze(1),
                                        res[:, bass.ds(g * G + b, 1), :], ALU.add).then_inc(M["xpost_ready"], 1)

            def statistics(kind, b, g, job):
                dve.wait_ge(M["xpost_ready"], job + 1)
                nc.vector.bn_stats(st6[:, b, :], x_post[:, b, :]).then_inc(M["st_ready"], 1)
                dve.wait_ge(M["st_ready"], job + 1)
                dve.nop(nofuse=True)
                nc.vector.bn_aggr(mv[:, b, :], st6[:, b, :]).then_inc(M["mv_ready"], 1)
                dve.wait_ge(M["mv_ready"], job + 1)
                nc.vector.tensor_scalar(var_e[:, b, :], mv[:, b, 1:2], LN_EPS, None, ALU.add).then_inc(
                    M["var_ready"], 1)

            def standardise(kind, b, g, job):
                dve.wait_ge(M["rstd_ready"], job + 1)
                wait_reuse(dve, M["yg_ready"], job - 1)
                nc.vector.tensor_scalar(y_n[:, b, :], x_post[:, b, :], mv[:, b, 0:1], rstd[:, b, :], ALU.subtract,
                                        ALU.mult).then_inc(M["yn_ready"], 1)

            def split_lo(i, name, kind):
                dve.wait_ge(M["hi_" + name], (i - (NEXT if kind == "s" else SELF)) + 1)
                for side, at, c in (("q", 0, C_SQB if kind == "s" else C_CQB),
                                    ("k", G * S, C_SKB if kind == "s" else C_CKB)):
                    key = kind + side
                    n = lo[key].shape[2]
                    last = nc.vector.scalar_tensor_tensor(
                        lo[key][:], proj_ps[bank_of(name)][:, at:at + G * n].rearrange("p (b n) -> p b n", b=G),
                        col(c), hi[key][:], ALU.add, ALU.subtract)
                last.then_inc(read(name), 1)

            def widen(i, name):
                key, b = name[:2], int(name[2])
                wait_read(dve, i, name)
                for j in range(RH):
                    last = nc.vector.tensor_scalar(wide[name[0]][:, b, j, :, :], rows_qk[key][:, b, :, :],
                                                   row_is_j[:, j:j + 1], None, ALU.mult)
                last.then_inc(M["wide_" + name[0]], 1)

            def store_v(i, name, kind, bias):
                n = KLEN[kind]
                if static(i) and i == NEXT:
                    dve.wait_ge(M["rows_in"], 16)
                wait_full(dve, i, name)
                wait_reuse(dve, M["av_ready"], UNITS * job_index(i, 2 if kind == "s" else 0))
                src = proj_ps[bank_of(name)][0:n, 0:G * D].rearrange("k (b a h d) -> k a b h d", b=G, a=2, d=HD)
                vb = row_sb[0:n, bias, :].rearrange("k (a h d) -> k a h d", a=2, d=HD)
                for a in range(2):
                    dst = v_aug[kind][:, :, 2 * a:2 * a + 2, :, 9 * a:9 * a + HD].rearrange(
                        "k b rr r d -> k b (rr r) d")
                    last = nc.vector.tensor_tensor(
                        dst, src[:, a], vb[:, a].unsqueeze(1).to_broadcast([n, G, 2 * RH, HD]), ALU.add)
                last.then_inc(read(name), 1)

            def norm_stats(src, st, mom, var, names, g):
                s_st, s_mv, s_var = names
                for b in range(G):
                    last = nc.vector.bn_stats(st[:, b, :], src[:, b, :])
                last.then_inc(M[s_st], 1)
                dve.wait_ge(M[s_st], g + 1)
                dve.nop(nofuse=True)
                for b in range(G):
                    last = nc.vector.bn_aggr(mom[:, b, :], st[:, b, :])
                last.then_inc(M[s_mv], 1)
                dve.wait_ge(M[s_mv], g + 1)
                nc.vector.tensor_scalar(var[:], mom[:, :, 1], LN_EPS, None, ALU.add).then_inc(M[s_var], 1)

            def light_work(i, k, u):
                g = i - TAIL
                for name in uses_at(i, k, u - 1):
                    if is_spread(name) and name[1] == "q":
                        widen(i, name)
                for name in uses_at(i, k, u):
                    if name in ("sqk", "cqk"):
                        split_lo(i, name, name[0])
                if (k, u) == (0, 1) and on(i, CROSS):
                    store_v(i, "cv", "c", R_CVB)
                if (k, u) == (1, 0) and on(i, TAIL):
                    dve.wait_ge(M["cn_loaded"], 16 * (g + 1))
                    nc.vector.tensor_scalar(e_k[:], cn_in[:, :, 0:D], 0.0, None, ALU.min).then_inc(M["mink_ready"], 1)
                if (k, u) == (1, 2) and on(i, TAIL):
                    dve.wait_ge(M["expk_ready"], g + 1)
                    nc.vector.scalar_tensor_tensor(phi_k[:], e_k[:], 1.0, cn_in[:, :, 0:D], ALU.subtract,
                                                   ALU.max).then_inc(M["phik_ready"], 1)
                if (k, u) == (1, 4) and on(i, TAIL):
                    wait_full(dve, i, "ff")
                    dve.wait_ge(M["res_ready"], job_index(i, 0))
                    nc.vector.tensor_tensor(x3[:], proj_ps[bank_of("ff")][:, 0:G * D].rearrange("p (b d) -> p b d", b=G),
                                            r2[:, bass.ds(g * G, G), :], ALU.add).then_inc(read("ff"), 1)
                if (k, u) == (2, 0) and on(i, TAIL):
                    wait_read(dve, i, "ff")
                    norm_stats(x3, st6_f, mv_f, var_f, ("st3_ready", "mv3_ready", "var3_ready"), g)
                if (k, u) == (2, 4) and on(i, NEXT):
                    store_v(i, "sv", "s", R_SVB)
                if (k, u) == (2, 2) and on(i, TAIL):
                    dve.wait_ge(M["rstd3_ready"], g + 1)
                    wait_reuse(dve, M["y3g_ready"], g)
                    for b in range(G):
                        last = nc.vector.tensor_scalar(y3[:, b, :], x3[:, b, :], mv_f[:, b, 0:1], rstd_f[:, b:b + 1],
                                                       ALU.subtract, ALU.mult)
                    last.then_inc(M["y3_ready"], 1)
                if (k, u) == (3, 0) and on(i, TAIL):
                    wait_read(dve, i, "yt")
                    nc.vector.tensor_scalar(e_q[:], x3_t[:], 0.0, None, ALU.min).then_inc(M["minq_ready"], 1)
                if (k, u) == (3, 1) and on(i, TAIL):
                    dve.wait_ge(M["expq_ready"], g + 1)
                    nc.vector.scalar_tensor_tensor(phi_q[:], e_q[:], 1.0, x3_t[:], ALU.subtract, ALU.max).then_inc(
                        M["phiq_ready"], 1)
                if (k, u) == (3, 4) and on(i, TAIL):
                    wait_full(dve, i, "la")
                    la = proj_ps[bank_of("la")][:, 0:G * (D + 1)].rearrange("p (b n) -> p b n", b=G)
                    nc.vector.tensor_scalar(den[:], la[:, :, D], DEN_EPS, None, ALU.add).then_inc(M["den_ready"], 1)
                    dve.wait_ge(M["den_ready"], g + 1)
                    nc.vector.reciprocal(rec4[:], den[:]).then_inc(M["rec4_ready"], 1)
                    dve.wait_ge(M["rec4_ready"], g + 1)
                    dve.wait_ge(M["r3_ready"], g + 1)
                    for b in range(G):
                        last = nc.vector.scalar_tensor_tensor(x4[:, b, :].unsqueeze(1), la[:, b:b + 1, 0:D],
                                                              rec4[:, b:b + 1], r3[:, bass.ds(g * G + b, 1), :],
                                                              ALU.mult, ALU.add)
                    last.then_inc(read("la"), 1)
                if (k, u) == (1, 0) and on(i, LAST):
                    wait_read(dve, i - 1, "la")
                    norm_stats(x4, st6_l, mv_l, var_l, ("st4_ready", "mv4_ready", "var4_ready"), i - LAST)
                if (k, u) == (1, 3) and on(i, LAST):
                    first = (i - LAST) * G
                    for b in range(G):
                        last = nc.vector.scalar_tensor_tensor(y4[:, b, :], x4[:, b, :], mv_l[:, b, 0:1],
                                                              row_sb[:, R_GAM, :], ALU.subtract, ALU.mult)
                    last.then_inc(M["y4_ready"], 1)
                    dve.wait_ge(M["y4_ready"], i - LAST + 1)
                    dve.wait_ge(M["rstd4_ready"], i - LAST + 1)
                    for b in range(G):
                        last = nc.vector.scalar_tensor_tensor(
                            o_all[:, bass.ds(first + b, 1), :], y4[:, b, :].unsqueeze(1), rstd_l[:, b:b + 1],
                            row_sb[:, R_BET:R_BET + 1, :], ALU.mult, ALU.add)
                    last.then_inc(M["out_ready"], 1)

            def iteration(i):
                if static(i) and i == SELF:
                    dve.wait_ge(M["r0_ready"], 1)
                for k in range(4):
                    cur, nxt, prev, prev_y = schedule(i, k)
                    for u in range(UNITS):
                        if nxt:
                            for ahead in maxima_at(u):
                                max_unit(*nxt, ahead)
                            if u == UNITS - 2:
                                split_max(*nxt)
                            if u == UNITS - 1:
                                widen_max(*nxt)
                        if u == 3 and prev:
                            standardise(*prev)
                        light_work(i, k, u)
                        if u == 0 and prev:
                            normalise(*prev)
                        if u == 2 and prev:
                            residual(*prev)
                            statistics(*prev)
                    light_work(i, k, UNITS)

            run_iterations(dve, iteration)

        @block.gpsimd
        def _(pool):
            nc.gpsimd.memset(neg_half[:], -0.5).then_inc(M["half_set"], 1)
            pool.wait_ge(M["half_set"], 1)
            pool.wait_ge(M["rows_in"], 16)
            pool.wait_ge(M["xall_in"], 16)

            def row(r, n):
                return row_sb[:, r:r + 1, :].to_broadcast([P, n, P])

            nc.gpsimd.tensor_tensor(r0[:], x_all[:], row(R_SOB, B), ALU.add).then_inc(M["r0_ready"], 1)
            nc.gpsimd.tensor_tensor(res_bias[:, 0, :], row_sb[:, R_E1, :], row_sb[:, R_COB, :], ALU.add)
            nc.gpsimd.tensor_tensor(res_bias[:, 1, :], row_sb[:, R_E2, :], row_sb[:, R_B2, :], ALU.add).then_inc(
                M["resb_set"], 1)
            pool.wait_ge(M["resb_set"], 1)

            def inverse_root(kind, b, g, job):
                pool.wait_ge(M["var_ready"], job + 1)
                nc.gpsimd.tensor_tensor(rstd[:, b, :], var_e[:, b, :], neg_half[:, 0:1], ALU.pow).then_inc(
                    M["rstd_ready"], 1)

            def next_residual(kind, b, g, job):
                gain, n, res = (R_G1, 0, r1) if kind == "s" else (R_G2, 1, r2)
                pool.wait_ge(M["yn_ready"], job + 1)
                nc.gpsimd.tensor_tensor(y_g[:], y_n[:, b, :], row_sb[:, gain, :], ALU.mult).then_inc(M["yg_ready"], 1)
                pool.wait_ge(M["yg_ready"], job + 1)
                nc.gpsimd.tensor_tensor(res[:, bass.ds(g * G + b, 1), :], y_g[:].unsqueeze(1),
                                        res_bias[:, n:n + 1, :], ALU.add).then_inc(M["res_ready"], 1)

            def iteration(i):
                g = i - TAIL
                for k in range(4):
                    cur, nxt, prev, prev_y = schedule(i, k)
                    if k == 1 and on(i, LAST):
                        pool.wait_ge(M["var4_ready"], i - LAST + 1)
                        nc.gpsimd.tensor_tensor(rstd_l[:], var_l[:], neg_half[:], ALU.pow).then_inc(
                            M["rstd4_ready"], 1)
                    if k == 2 and on(i, TAIL):
                        pool.wait_ge(M["var3_ready"], g + 1)
                        nc.gpsimd.tensor_tensor(rstd_f[:], var_f[:], neg_half[:], ALU.pow).then_inc(
                            M["rstd3_ready"], 1)
                    if prev:
                        inverse_root(*prev)
                        next_residual(*prev)
                    if k == 2 and on(i, TAIL):
                        pool.wait_ge(M["y3_ready"], g + 1)
                        nc.gpsimd.tensor_tensor(y3_g[:], y3[:], row(R_G3, G), ALU.mult).then_inc(M["y3g_ready"], 1)
                        pool.wait_ge(M["y3g_ready"], g + 1)
                        nc.gpsimd.tensor_tensor(r3[:, bass.ds(g * G, G), :], y3_g[:], row(R_E3, G), ALU.add).then_inc(
                            M["r3_ready"], 1)

            run_iterations(pool, iteration)


def kernel(**inputs):
    import numpy as np
    import concourse.bacc as bacc
    from concourse.bass_utils import run_bass_kernel_spmd

    a = {k.replace("L0_xattn_", "").replace("L1_xattn_", ""): np.asarray(v) for k, v in inputs.items()}
    x, c, mask = a["x"], a["ctx_1024"], a["mask_1x1xSxS_ik0"][0, 0]
    b, s, d = x.shape
    sk = c.shape[1]
    square = ["sa_qw", "sa_kw", "sa_vw", "sa_ow", "ca_qw", "ca_kw", "ca_vw", "ca_ow"]
    nf = a["w1"].shape[1] // P
    blocks = [a[n] for n in square] + [a["w1"][:, P * n:P * n + P] for n in range(nf)] + \
             [a["w2"][P * n:P * n + P] for n in range(nf)]
    columns = [a["sa_qb"], a["sa_kb"], a["ca_qb"], a["ca_kb"]] + [a["b1"][P * n:P * n + P] for n in range(nf)] + \
              [a[n] for n in ("g1", "be1", "g2", "be2", "g3", "be3")]
    rows = [a[n] for n in ("sa_vb", "sa_ob", "ca_vb", "ca_ob", "b2", "g1", "be1", "g2", "be2", "g3", "be3", "gamma",
                           "beta")]
    data = {
        "x": x,
        "x_t": x.reshape(b // G, G, s, d).transpose(0, 3, 1, 2),
        "ctx_n": c,
        "ctx_t": c.reshape(b // G, G, sk, d).transpose(0, 3, 1, 2),
        "mask_q": mask,
        "mask_k": mask.T,
        "weights": np.stack(blocks, axis=1),
        "cols": np.stack(columns, axis=1),
        "rows": np.stack(rows),
        "ident": np.eye(P, dtype=np.float32),
    }
    data = {n: np.ascontiguousarray(v) for n, v in data.items()}
    nc = bacc.Bacc("TRN2", target_bir_lowering=False, num_devices=1)
    args = [nc.dram_tensor("in_" + n, v.shape, mybir.dt.from_np(v.dtype), kind="ExternalInput").ap()
            for n, v in data.items()]
    out = nc.dram_tensor("out", (b, s, d), F32, kind="ExternalOutput").ap()
    decoder_layer_kernel(nc, *args, out)
    r = run_bass_kernel_spmd(nc, [{"in_" + n: v for n, v in data.items()}], core_ids=[0])
    return r.results[0]["out"]
```
